# Optimizing a Trainium2 kernel written in Bass

```python
import numpy as np
import jax
import jax.numpy as jnp

def _softmax(x, axis=-1):
    return jax.nn.softmax(x, axis=axis)

def _gelu(x):
    return jax.nn.gelu(x, approximate=True)

def _silu(x):
    return jax.nn.silu(x)

def _sigmoid(x):
    return jax.nn.sigmoid(x)

def _layernorm(x, axis=-1, eps=1e-05):
    m = jnp.mean(x, axis=axis, keepdims=True)
    v = jnp.var(x, axis=axis, keepdims=True)
    return (x - m) / jnp.sqrt(v + eps)

def _scatter_add(tgt, idx, src, axis=0):
    return tgt.at[idx].add(src)

def _segment_sum(src, seg, n):
    return jax.ops.segment_sum(src, seg, n)
kernel_name = 'mk_gnn_ffn_d1_gnn_r8_3144df'

def setup_inputs(seed: int=0):
    np.random.seed(seed)
    _w = jnp.asarray

    def _rec_inputs():
        import jax
        import jax.numpy as jnp
        _gk = jax.random.key(seed)
        x = -0.0002117 + 1 * jax.random.normal(jax.random.fold_in(_gk, 1), (6250, 512), jnp.float32)
        src = jax.random.randint(jax.random.fold_in(_gk, 2), (100000,), 0, 6250, jnp.int32)
        dst = jnp.minimum((6250 * jax.random.uniform(jax.random.fold_in(_gk, 3), (100000,)) ** 2.0).astype(jnp.int32), 49999)
        _o = jnp.argsort(dst, stable=True)
        src = src[_o]
        dst = dst[_o]
        return (x, src, dst)
    x, src, dst = _rec_inputs()

    def _L0_gnn_setup():
        import jax, jax.numpy as jnp
        import numpy as np
        N = 6250
        E = 50000
        IN_FEATS = 512
        HEADS = 8
        OUT_FEATS = 64
        NEG_SLOPE = 0.2
        key = jax.random.key(seed)
        ks = jax.random.split(key, 12)
        HF = HEADS * OUT_FEATS
        s = 1.0 / np.sqrt(IN_FEATS)
        inp = {'feat': jax.random.normal(ks[0], (N, IN_FEATS), dtype=jnp.float32), 'src': jax.random.randint(ks[1], (E,), 0, N, dtype=jnp.int32), 'dst': jax.random.randint(ks[2], (E,), 0, N, dtype=jnp.int32), 'W_src': jax.random.normal(ks[3], (IN_FEATS, HF), dtype=jnp.float32) * s, 'b_src': jax.random.normal(ks[4], (HF,), dtype=jnp.float32) * 0.01, 'W_dst': jax.random.normal(ks[5], (IN_FEATS, HF), dtype=jnp.float32) * s, 'b_dst': jax.random.normal(ks[6], (HF,), dtype=jnp.float32) * 0.01, 'W_val': jax.random.normal(ks[7], (IN_FEATS, HF), dtype=jnp.float32) * s, 'b_val': jax.random.normal(ks[8], (HF,), dtype=jnp.float32) * 0.01, 'attn_l': jax.random.normal(ks[9], (HEADS, OUT_FEATS), dtype=jnp.float32) * 0.1, 'attn_r': jax.random.normal(ks[10], (HEADS, OUT_FEATS), dtype=jnp.float32) * 0.1}
        return inp
    _L0_gnn_all = _L0_gnn_setup()
    _L0_gnn_in = {k: v for k, v in _L0_gnn_all.items() if k in ('W_src', 'b_src', 'W_dst', 'b_dst', 'W_val', 'b_val', 'attn_l', 'attn_r')}
    del _L0_gnn_all

    def _L0_ffn_setup():
        import jax, jax.numpy as jnp
        import numpy as np
        B, S, D = (8, 512, 512)
        H = 256
        O = 512
        E = 8
        TOP_K = 1
        key = jax.random.key(seed)
        ks = jax.random.split(key, 8)
        sc = 0.02
        return {'x': jax.random.normal(ks[0], (B, S, D), dtype=jnp.float32), 'Wr': jax.random.normal(ks[1], (D, E), dtype=jnp.float32) * sc, 'br': jnp.zeros((E,), dtype=jnp.float32), 'W1': jax.random.normal(ks[2], (E, D, H), dtype=jnp.float32) * sc, 'b1': jnp.zeros((E, H), dtype=jnp.float32), 'W2': jax.random.normal(ks[3], (E, H, O), dtype=jnp.float32) * sc, 'b2': jnp.zeros((E, O), dtype=jnp.float32)}
    _L0_ffn_all = _L0_ffn_setup()
    _L0_ffn_in = {k: v for k, v in _L0_ffn_all.items() if k in ('Wr', 'br', 'W1', 'b1', 'W2', 'b2')}
    del _L0_ffn_all
    return {'x': x, 'src': src, 'dst': dst, 'L0_gnn_W_src': _L0_gnn_in['W_src'], 'L0_gnn_b_src': _L0_gnn_in['b_src'], 'L0_gnn_W_dst': _L0_gnn_in['W_dst'], 'L0_gnn_b_dst': _L0_gnn_in['b_dst'], 'L0_gnn_W_val': _L0_gnn_in['W_val'], 'L0_gnn_b_val': _L0_gnn_in['b_val'], 'L0_gnn_attn_l': _L0_gnn_in['attn_l'], 'L0_gnn_attn_r': _L0_gnn_in['attn_r'], 'L0_ffn_Wr': _L0_ffn_in['Wr'], 'L0_ffn_br': _L0_ffn_in['br'], 'L0_ffn_W1': _L0_ffn_in['W1'], 'L0_ffn_b1': _L0_ffn_in['b1'], 'L0_ffn_W2': _L0_ffn_in['W2'], 'L0_ffn_b2': _L0_ffn_in['b2']}

def reference(x, src, dst, L0_gnn_W_src, L0_gnn_b_src, L0_gnn_W_dst, L0_gnn_b_dst, L0_gnn_W_val, L0_gnn_b_val, L0_gnn_attn_l, L0_gnn_attn_r, L0_ffn_Wr, L0_ffn_br, L0_ffn_W1, L0_ffn_b1, L0_ffn_W2, L0_ffn_b2):
    import jax
    import jax.numpy as jnp

    def _L0_gnn_ref(feat, src, dst, W_src, b_src, W_dst, b_dst, W_val, b_val, attn_l, attn_r):
        import jax, jax.numpy as jnp
        import numpy as np
        N = 6250
        E = 50000
        IN_FEATS = 512
        HEADS = 8
        OUT_FEATS = 64
        NEG_SLOPE = 0.2
        feat_src = (feat @ W_src + b_src).reshape(N, HEADS, OUT_FEATS)
        feat_dst = (feat @ W_dst + b_dst).reshape(N, HEADS, OUT_FEATS)
        feat_v = (feat @ W_val + b_val).reshape(N, HEADS, OUT_FEATS)
        el = jnp.einsum('nhf,hf->nh', feat_src, attn_l)
        er = jnp.einsum('nhf,hf->nh', feat_dst, attn_r)
        e = el[src] + er[dst]
        e = jnp.where(e >= 0, e, NEG_SLOPE * e)
        e_max = jax.ops.segment_max(e, dst, num_segments=N)
        e_max = jnp.where(jnp.isfinite(e_max), e_max, 0.0)
        exp_e = jnp.exp(e - e_max[dst])
        denom = jax.ops.segment_sum(exp_e, dst, num_segments=N)
        a = exp_e / jnp.maximum(denom[dst], 1e-16)
        msg = feat_v[src] * a[:, :, None]
        rst = jax.ops.segment_sum(msg, dst, num_segments=N)
        return rst.reshape(N, HEADS * OUT_FEATS)

    def _L0_ffn_ref(x, Wr, br, W1, b1, W2, b2):
        import jax, jax.numpy as jnp
        import numpy as np
        B, S, D = (8, 512, 512)
        H = 256
        O = 512
        E = 8
        TOP_K = 1
        b, s, d = x.shape
        xf = x.reshape(-1, d)
        router_logits = xf @ Wr + br
        topk_logits, topk_idx = jax.lax.top_k(router_logits, TOP_K)
        topk_gates = jax.nn.softmax(topk_logits, axis=1)
        out = jnp.zeros((xf.shape[0], O), dtype=x.dtype)
        for k in range(TOP_K):
            idx_k = topk_idx[:, k]
            gate_k = topk_gates[:, k:k + 1]
            for e in range(E):
                h = jax.nn.relu(xf @ W1[e] + b1[e])
                oe = h @ W2[e] + b2[e]
                mask = (idx_k == e)[:, None]
                out = out + jnp.where(mask, gate_k * oe, 0.0)
        return out.reshape(b, s, O)
    x = x + _L0_gnn_ref(_layernorm(x, axis=-1), src, dst, L0_gnn_W_src, L0_gnn_b_src, L0_gnn_W_dst, L0_gnn_b_dst, L0_gnn_W_val, L0_gnn_b_val, L0_gnn_attn_l, L0_gnn_attn_r)
    x = x + _L0_ffn_ref(_layernorm(x, axis=-1)[None], L0_ffn_Wr, L0_ffn_br, L0_ffn_W1, L0_ffn_b1, L0_ffn_W2, L0_ffn_b2)[0]
    return x

_drawn_inputs = setup_inputs


def setup_inputs(seed=0):
    import zlib

    import numpy as np

    out = dict(_drawn_inputs(seed))
    spreads = {'L0_ffn_br': (0.0, 0.1), 'L0_ffn_b1': (0.0, 0.393), 'L0_ffn_b2': (0.0, 0.1)}
    factors = {'L0_gnn_b_src': 43.914, 'L0_gnn_b_dst': 43.316, 'L0_gnn_b_val': 3.612}
    for name, (base, spread) in spreads.items():
        noise = np.random.default_rng([zlib.crc32(name.encode()), seed]).standard_normal(out[name].shape)
        drawn = base * np.exp(spread * noise) if base else spread * noise
        out[name] = jnp.asarray(drawn.astype(out[name].dtype))
    for name, factor in factors.items():
        out[name] = (out[name] * factor).astype(out[name].dtype)
    return out
```

```python
from contextlib import ExitStack

import concourse.bass as bass
from concourse import mybir

F32 = mybir.dt.float32
BF16 = mybir.dt.bfloat16
I32 = mybir.dt.int32
ALU = mybir.AluOpType
ACT = mybir.ActivationFunctionType
AX_X = mybir.AxisListType.X
RMAX = bass.bass_isa.ReduceOp.max

P = 128
N = 6250
E = 100000
D = 512
KC = D // P
H = 8
HD = D // H
NT = -(-N // P)
NLAST = N - (NT - 1) * P
ET = 784
EPAD = ET * P
STEPS = ET + NT - 1
G = 4
NG = STEPS // G
Q = 4
PASS = G * Q
NPASS = STEPS // PASS
SCH = 7
ROW = D + H
NX = 8
HID = 256
FT = NT + NX - 1
XROW = D + 2
NEG_SLOPE = 0.2
LN_EPS = 1e-5
FAR = 1 << 20
assert STEPS == NPASS * PASS and SCH * P >= STEPS + 2 * G and EPAD >= E


class Chain:

    def __init__(self, eng, sem):
        self.eng, self.sem, self.n, self.made = eng, sem, 0, 0

    def __call__(self, ins):
        ins.then_inc(self.sem, 1)
        self.n, self.made = self.n + 1, self.made + 1
        self.eng.wait_ge(self.sem, self.n)


def wait(eng, sem, value):
    if not isinstance(value, int) or value > 0:
        eng.wait_ge(sem, value)


def looped(eng, chain, trips, body):
    start = chain.made if chain else 0
    body(0)
    per = chain.made - start if chain else 0
    base = chain.n if chain else 0
    with eng.Fori(1, trips) as k:
        if chain:
            chain.n = base + (k - 1) * per
        body(k)
    if chain:
        assert chain.made - start == 2 * per
        chain.n = base + (trips - 1) * per


def carry_wait(dve, c):
    dve.tensor_scalar(c.junk[:, 0:1], c.junk[:, 1:2], 1.0, None, ALU.mult)


def tensors(nc, ctx, tag):
    sb = lambda name, shape, dt=F32: ctx.enter_context(nc.sbuf_tensor(f"{tag}_{name}", shape, dt))
    ps = lambda name, shape, dt=F32: ctx.enter_context(nc.psum_tensor(f"{tag}_ps_{name}", shape, dt))
    sem = lambda name: ctx.enter_context(nc.semaphore(f"{tag}_{name}"))
    return sb, ps, sem


def constants(nc, c):
    with ExitStack() as ctx:
        _, _, sem = tensors(nc, ctx, "cst")
        made, ordered = sem("made"), sem("ordered")
        block = ctx.enter_context(nc.Block())

        @block.gpsimd
        def _(pool):
            pool.iota(c.lane_i[:, :], pattern=[[1, P]], base=0, channel_multiplier=0).then_inc(made, 1)
            pool.iota(c.part_i[:, :], pattern=[[0, 1]], base=0, channel_multiplier=1).then_inc(made, 1)
            pool.iota(c.step_i[:, :], pattern=[[P, SCH]], base=0, channel_multiplier=1).then_inc(made, 1)
            pool.iota(c.count_i[:, :], pattern=[[1, STEPS + 1]], base=0, channel_multiplier=0).then_inc(made, 1)

        @block.vector
        def _(dve):
            link = Chain(dve, ordered)
            dve.wait_ge(made, 4)
            dve.tensor_copy(c.step[:, :], c.step_i[:, :])
            dve.tensor_copy(c.count[:, :], c.count_i[:, :])
            dve.memset(c.ones[:, :], 1.0)
            dve.memset(c.zeros_bf[:, :], 0.0)
            dve.memset(c.junk[:, :], 0.0)
            dve.memset(c.eps[:, :], LN_EPS)
            link(dve.tensor_copy(c.lane[:, :], c.lane_i[:, :]))
            link(dve.tensor_copy(c.part[:, :], c.part_i[:, :]))
            dve.tensor_scalar(c.ident[:, :], c.lane[:, :], c.part[:, 0:1], None, ALU.is_equal)
            dve.tensor_scalar(c.upper[:, :], c.lane[:, :], c.part[:, 0:1], None, ALU.is_gt)


def node_phase(nc, c, x, W_src, b_src, W_dst, b_dst, W_val, b_val, attn_l, attn_r, table):
    with ExitStack() as ctx:
        sb, ps, sem = tensors(nc, ctx, "nod")
        wval = sb("wval", [P, KC, D])
        wlog = sb("wlog", [P, 2, KC, D])
        attn = sb("attn", [P, 2, D])
        bias = sb("bias", [P, 3, D])
        wel = sb("wel", [P, KC, 2, H])
        bel = sb("bel", [P, 2, H])
        xt = sb("xt", [P, 2, D])
        stats = sb("stats", [P, 2, 6])
        mv = sb("mv", [P, 2, 2])
        std = sb("std", [P, 2, 1])
        rstd = sb("rstd", [P, 2, 1])
        xn = sb("xn", [P, 2, D])
        xT = sb("xT", [P, 2, D])
        row = sb("row", [P, 2, ROW])
        ps_t = [ps(f"t{i}", [P, D]) for i in range(2)]
        ps_v = [ps(f"v{i}", [P, D]) for i in range(2)]
        ps_e = [ps(f"e{i}", [P, 2 * H]) for i in range(2)]
        weights_in, weights_ready = sem("weights_in"), sem("weights_ready")
        x_in = [sem(f"x_in{i}") for i in range(2)]
        row_out = [sem(f"row_out{i}") for i in range(2)]
        moments, std_ready, xn_ready = sem("moments"), sem("std_ready"), sem("xn_ready")
        transposed, copied, projected, row_ready = sem("transposed"), sem("copied"), sem("projected"), sem("row_ready")
        ordered = sem("ordered")
        block = ctx.enter_context(nc.Block())

        @block.sync
        def _(sp):
            sp.dma_start(wval[:, :, :], W_val.rearrange("(k p) n -> p k n", p=P)).then_inc(weights_in, 16)
            sp.dma_start(wlog[:, 0], W_src.rearrange("(k p) n -> p k n", p=P)).then_inc(weights_in, 16)
            sp.dma_start(wlog[:, 1], W_dst.rearrange("(k p) n -> p k n", p=P)).then_inc(weights_in, 16)
            for i, a in enumerate((attn_l, attn_r)):
                sp.dma_start(attn[:, i], a.rearrange("(o h) f -> o (h f)", o=1).broadcast_to([P, D])).then_inc(weights_in, 16)
            for i, b in enumerate((b_val, b_src, b_dst)):
                sp.dma_start(bias[:, i], b.rearrange("(o n) -> o n", o=1).broadcast_to([P, D])).then_inc(weights_in, 16)

            def load(i, s, turn, rows=P):
                wait(sp, xn_ready, i - 1)
                sp.dma_start(xt[0:rows, s], x[bass.ds(i * P, rows), :]).then_inc(x_in[s], 16)

            def store(i, s):
                sp.wait_ge(row_ready, i + 1)
                sp.dma_start(table[bass.ds(i * P, P), :], row[:, s]).then_inc(row_out[s], 16)

            load(0, 0, 0)

            def two(k):
                for s in range(2):
                    if s == 0:
                        load(2 * k + 1, 1, k)
                    else:
                        load(2 * k + 2, 0, k)
                    store(2 * k + s, s)

            load_last = NT - 1
            two(0)
            with sp.Fori(1, NT // 2 - 1) as k:
                two(k)
            k = NT // 2 - 1
            load(2 * k + 1, 1, k)
            store(2 * k, 0)
            load(load_last, 0, k, NLAST)
            store(2 * k + 1, 1)
            store(NT - 1, 0)
            sp.wait_ge(row_out[0], 16 * (NT // 2 + 1))
            sp.wait_ge(row_out[1], 16 * (NT // 2))

        @block.vector
        def _(dve):
            link = Chain(dve, ordered)
            dve.wait_ge(weights_in, 16 * 8)
            for i in range(2):
                for k in range(KC):
                    link(dve.tensor_tensor(wlog[:, i, k], wlog[:, i, k], attn[:, i], ALU.mult))
                link(dve.tensor_tensor(bias[:, 1 + i], bias[:, 1 + i], attn[:, i], ALU.mult))
                for k in range(KC):
                    link(dve.tensor_reduce(wel[:, k, i], wlog[:, i, k].rearrange("p (h f) -> p h f", h=H), AX_X, ALU.add))
                ins = dve.tensor_reduce(bel[:, i], bias[:, 1 + i].rearrange("p (h f) -> p h f", h=H), AX_X, ALU.add)
                link(ins)
            dve.engine_nop().then_inc(weights_ready, 1)

            def normalise(i, s, turn):
                dve.wait_ge(x_in[s], 16 * (turn + 1))
                link(dve.bn_stats(stats[:, s], xt[:, s]))
                carry_wait(dve, c)
                dve.bn_aggr(mv[:, s], stats[:, s]).then_inc(moments, 1)
                dve.wait_ge(moments, i + 1)
                dve.wait_ge(std_ready, i + 1)
                link(dve.reciprocal(rstd[:, s], std[:, s]))
                wait(dve, transposed, i - 1)
                dve.tensor_scalar(xn[:, s], xt[:, s], mv[:, s, 0:1], rstd[:, s], ALU.subtract, ALU.mult).then_inc(xn_ready, 1)

            def evacuate(i, s, turn):
                dve.wait_ge(projected, i + 1)
                wait(dve, row_out[s], 16 * turn)
                link(dve.tensor_tensor(c.logit[:, bass.ds(i * 2 * H, 2 * H)], ps_e[s][:, :],
                                       bel[:, :, :].rearrange("p a h -> p (a h)"), ALU.add))
                dve.tensor_scalar(row[:, s, D:ROW], c.logit[:, bass.ds(i * 2 * H, H)], 1.0, None, ALU.mult)
                dve.tensor_tensor(row[:, s, 0:D], ps_v[s][:, :], bias[:, 0], ALU.add).then_inc(row_ready, 1)

            normalise(0, 0, 0)

            def two(k):
                normalise(2 * k + 1, 1, k)
                evacuate(2 * k, 0, k)
                normalise(2 * k + 2, 0, k + 1)
                evacuate(2 * k + 1, 1, k)

            looped(dve, link, NT // 2, two)
            evacuate(NT - 1, 0, NT // 2)

        @block.scalar
        def _(act):
            def root(i, s):
                act.wait_ge(moments, i + 1)
                act.activation(std[:, s], mv[:, s, 1:2], ACT.Sqrt, bias=c.eps[:, 0:1]).then_inc(std_ready, 1)

            def copy(i, s):
                act.wait_ge(transposed, i + 1)
                wait(act, projected, i - 1)
                act.copy(xT[:, s], ps_t[s][:, :]).then_inc(copied, 1)

            root(0, 0)
            copy(0, 0)

            def two(k):
                for s in (1, 0):
                    i = 2 * k + 1 + (s == 0)
                    root(i, s)
                    copy(i, s)

            looped(act, None, NT // 2, two)

        @block.tensor
        def _(pe):
            def transpose(i, s):
                pe.wait_ge(xn_ready, i + 1)
                wait(pe, copied, i - 1)
                for k in range(KC):
                    ins = pe.transpose(ps_t[s][:, k * P:(k + 1) * P], xn[:, s, k * P:(k + 1) * P], c.ident[:, :])
                ins.then_inc(transposed, 1)

            def project(i, s):
                pe.wait_ge(copied, i + 1)
                wait(pe, row_ready, i - 1)
                for k in range(KC):
                    pe.matmul(ps_v[s][:, :], xT[:, s, k * P:(k + 1) * P], wval[:, k], start=k == 0, stop=k == KC - 1)
                for k in range(KC):
                    ins = pe.matmul(ps_e[s][:, :], xT[:, s, k * P:(k + 1) * P],
                                    wel[:, k].rearrange("p a h -> p (a h)"), start=k == 0, stop=k == KC - 1)
                ins.then_inc(projected, 1)

            pe.wait_ge(weights_ready, 1)
            transpose(0, 0)

            def two(k):
                transpose(2 * k + 1, 1)
                project(2 * k, 0)
                transpose(2 * k + 2, 0)
                project(2 * k + 1, 1)

            looped(pe, None, NT // 2, two)
            project(NT - 1, 0)


def edge_phase(nc, c, src, dst, src_pad, dst_pad):
    with ExitStack() as ctx:
        sb, ps, sem = tensors(nc, ctx, "edg")
        pad = sb("pad", [1, 2, EPAD - E], I32)
        dst_i = sb("dst_i", [P, ET], I32)
        dst_f = sb("dst_f", [P, ET])
        below = sb("below", [P, NT, 1])
        scratch = sb("scratch", [P, ET])
        last_i = sb("last_i", [P, NT], I32)
        last = sb("last", [P, NT])
        lcol_i = sb("lcol_i", [NT, 1], I32)
        lcol = sb("lcol", [NT, 1])
        block_of = sb("block_of", [P, SCH, 1])
        tile_f = sb("tile_f", [P, SCH])
        tile_i = sb("tile_i", [P, SCH], I32)
        rows_i = sb("rows_i", [P, 2, SCH, P], I32)
        rows_f = sb("rows_f", [P, 2, SCH, P])
        passed = sb("passed", [NT, STEPS + 1])
        brow = sb("brow", [1, STEPS + 1])
        bits = sb("bits", [1, 1, PASS])
        bits_i = sb("bits_i", [1, PASS], I32)
        flag = sb("flag", [1, NPASS, PASS])
        word = sb("word", [1, NPASS])
        top = sb("top", [P, 2, H])
        gtop = sb("gtop", [P, 2, H])
        z = sb("z", [P, NT, H])
        z2 = sb("z2", [P, NT, H])
        rest = sb("rest", [P, NT * 2 * H])
        ps_c = ps("c", [P, NT])
        ps_l = ps("l", [NT, 1])
        ps_b = ps("b", [1, 2, 512])
        ps_r = [ps(f"r{i}", [P, P]) for i in range(2)]
        pads_ready, padded, dst_in = sem("pads_ready"), sem("padded"), sem("dst_in")
        counted, summed, tiles_ready = sem("counted"), sem("summed"), sem("tiles_ready")
        rows_in, rows_ready = sem("rows_in"), sem("rows_ready")
        passed_ready, brow_done = sem("passed_ready"), sem("brow_done")
        turned, kept, ordered = sem("turned"), sem("kept"), sem("ordered")
        tops_ready, tops_all = sem("tops_ready"), sem("tops_all")
        block = ctx.enter_context(nc.Block())

        @block.sync
        def _(sp):
            sp.dma_start(src_pad[0:E].rearrange("(a b) -> a b", b=800), src.rearrange("(a b) -> a b", b=800)).then_inc(padded, 16)
            sp.dma_start(dst_pad[0:E].rearrange("(a b) -> a b", b=800), dst.rearrange("(a b) -> a b", b=800)).then_inc(padded, 16)
            sp.wait_ge(pads_ready, 2)
            sp.dma_start(src_pad[E:EPAD].rearrange("(o n) -> o n", o=1), pad[:, 0]).then_inc(padded, 16)
            sp.dma_start(dst_pad[E:EPAD].rearrange("(o n) -> o n", o=1), pad[:, 1]).then_inc(padded, 16)
            sp.wait_ge(padded, 64)
            sp.dma_start(dst_i[:, :], dst_pad.rearrange("(p n) -> p n", p=P)).then_inc(dst_in, 16)

        @block.gpsimd
        def _(pool):
            pool.memset(pad[:, 0], 0).then_inc(pads_ready, 1)
            pool.memset(pad[:, 1], FAR).then_inc(pads_ready, 1)
            pool.iota(bits_i[:, :], pattern=[[0, PASS]], base=0, channel_multiplier=0)
            pool.wait_ge(tops_ready, 2)
            pool.partition_all_reduce(gtop[:, :, :].rearrange("p a h -> p (a h)"),
                                      top[:, :, :].rearrange("p a h -> p (a h)"), P, RMAX).then_inc(tops_all, 1)
            pool.wait_ge(tiles_ready, 1)
            for which, pad_rows in enumerate((src_pad, dst_pad)):
                for ch in range(SCH):
                    pool.indirect_dma_start(
                        out=rows_i[:, which, ch], out_offset=None, in_=pad_rows.rearrange("(t e) -> t e", e=P),
                        in_offset=bass.IndirectOffsetOnAxis(ap=tile_i[:, ch:ch + 1], axis=0)).then_inc(rows_in, 16)
            pool.wait_ge(rows_in, 16 * 2 * SCH)

        @block.vector
        def _(dve):
            link = Chain(dve, ordered)
            el = c.logit[:, :].rearrange("p (t a h) -> p t a h", a=2, h=H)
            link(dve.tensor_reduce(top[:, 0], el[:, :, 0].rearrange("p t h -> p h t"), AX_X, ALU.max))
            link(dve.tensor_scalar(z[:, :, :], el[:, :, 0], -1.0, None, ALU.mult))
            dve.tensor_reduce(top[:, 1], z[:, :, :].rearrange("p t h -> p h t"), AX_X, ALU.max).then_inc(tops_ready, 2)
            dve.wait_ge(tops_ready, 2)
            for j in range(PASS):
                dve.memset(bits[:, :, j:j + 1], float(64 << j))
            dve.wait_ge(dst_in, 16)
            link(dve.tensor_copy(dst_f[:, :], dst_i[:, :]))
            for b in range(NT):
                end = float(P * (b + 1)) if b < NT - 1 else float(2 * FAR)
                link(dve.tensor_scalar(scratch[:, :], dst_f[:, :], end, 0.0, ALU.is_lt, ALU.add, accum_out=below[:, b]))
            dve.engine_nop().then_inc(counted, 1)
            dve.wait_ge(summed, 1)
            for n, ints, out, add in ((ps_c[:, :], last_i[:, :], last[:, :], c.count[:, 0:NT]),
                                      (ps_l[:, :], lcol_i[:, :], lcol[:, :], c.part[0:NT, 0:1])):
                link(dve.tensor_scalar(out, n, -1.0, 0.0, ALU.add, ALU.max))
                link(dve.tensor_copy(ints, out))
                link(dve.tensor_scalar(ints, ints, 7, None, ALU.arith_shift_right))
                link(dve.tensor_copy(out, ints))
                link(dve.tensor_tensor(out, out, add, ALU.add))
            for ch in range(SCH):
                link(dve.tensor_scalar(scratch[:, 0:NT], last[:, :], c.step[:, ch:ch + 1], 0.0, ALU.is_lt, ALU.add,
                                       accum_out=block_of[:, ch]))
            link(dve.tensor_tensor(tile_f[:, :], c.step[:, :], block_of[:, :, 0], ALU.subtract))
            link(dve.tensor_scalar(tile_f[:, :], tile_f[:, :], float(ET - 1), None, ALU.min))
            dve.tensor_copy(tile_i[:, :], tile_f[:, :]).then_inc(tiles_ready, 1)
            dve.tensor_scalar(passed[:, :], c.count[0:NT, :], lcol[:, 0:1], None, ALU.is_gt).then_inc(passed_ready, 1)
            dve.wait_ge(brow_done, 1)
            link(dve.tensor_copy(brow[:, 0:512], ps_b[:, 0, :]))
            link(dve.tensor_copy(brow[:, 512:STEPS + 1], ps_b[:, 1, 0:STEPS + 1 - 512]))
            flags = flag[:, :, :].rearrange("o a b -> o (a b)")
            link(dve.tensor_tensor(flags, brow[:, 1:STEPS + 1], brow[:, 0:STEPS], ALU.subtract))
            link(dve.tensor_tensor(flag[:, :, :], flag[:, :, :], bits[:, :, :].broadcast_to([1, NPASS, PASS]), ALU.mult))
            link(dve.tensor_reduce(word[:, :], flag[:, :, :], AX_X, ALU.add))
            link(dve.tensor_tensor(word[:, :], word[:, :],
                                   brow[:, 0:STEPS].rearrange("o (a b) -> o a b", b=PASS)[:, :, 0], ALU.add))
            dve.memset(c.control[:, NPASS:NPASS + 1], 0)
            link(dve.tensor_copy(c.control[:, 0:NPASS], word[:, :]))
            dve.wait_ge(tops_all, 1)
            shift = el[:, :, 0]
            link(dve.tensor_tensor(z[:, :, :], el[:, :, 1], gtop[:, 0:1].broadcast_to([P, NT, H]), ALU.add))
            link(dve.scalar_tensor_tensor(shift, z[:, :, :], NEG_SLOPE, z[:, :, :], ALU.mult, ALU.max))
            link(dve.tensor_copy(rest[:, :], c.logit[:, :]))
            for part in range(3):
                link(dve.tensor_copy(c.logit3[:, part], rest[:, :]))
                if part < 2:
                    link(dve.tensor_tensor(rest[:, :], rest[:, :], c.logit3[:, part], ALU.subtract))
            dve.wait_ge(rows_in, 16 * 2 * SCH)
            link(dve.tensor_copy(rows_f[:, :, :, :], rows_i[:, :, :, :]))
            link(dve.tensor_scalar(block_of[:, :, :], block_of[:, :, :], float(P), None, ALU.mult))
            for ch in range(SCH):
                ins = dve.tensor_scalar(rows_f[:, 1, ch], rows_f[:, 1, ch], block_of[:, ch], None, ALU.subtract)
            link(ins)
            dve.engine_nop().then_inc(rows_ready, 1)
            for n in range(2 * SCH):
                dve.wait_ge(turned, n + 1)
                out = c.step_src if n < SCH else c.step_dst
                ch = n % SCH
                dve.tensor_copy(out[:, ch * P:(ch + 1) * P], ps_r[n % 2][:, :]).then_inc(kept, 1)

        @block.tensor
        def _(pe):
            pe.wait_ge(counted, 1)
            pe.matmul(ps_c[:, :], c.ones[:, :], below[:, :, 0], start=True, stop=True)
            pe.matmul(ps_l[:, :], below[:, :, 0], c.ones[:, 0:1], start=True, stop=True).then_inc(summed, 1)
            pe.wait_ge(passed_ready, 1)
            pe.matmul(ps_b[:, 0, :], c.ones[0:NT, 0:1], passed[:, 0:512], start=True, stop=True)
            pe.matmul(ps_b[:, 1, 0:STEPS + 1 - 512], c.ones[0:NT, 0:1], passed[:, 512:STEPS + 1],
                      start=True, stop=True).then_inc(brow_done, 1)
            pe.wait_ge(rows_ready, 1)
            for n in range(2 * SCH):
                wait(pe, kept, n - 1)
                pe.transpose(ps_r[n % 2][:, :], rows_f[:, n // SCH, n % SCH], c.ident[:, :]).then_inc(turned, 1)


def message_phase(nc, c, table, sums):
    with ExitStack() as ctx:
        sb, ps, sem = tensors(nc, ctx, "msg")
        index = sb("index", [P, Q, G], I32)
        rows = sb("rows", [P, Q, G, ROW])
        hot = sb("hot", [P, Q, G, P])
        hotT = sb("hotT", [P, 2, G, P], BF16)
        z = sb("z", [P, 2, G, H])
        z2 = sb("z2", [P, 2, G, H])
        weight = sb("weight", [P, 2, G, H])
        message = sb("message", [P, 2, G, D])
        out = sb("out", [P, 2 * ROW])
        junk = sb("junk", [1, Q + 1])
        ps_hot = [ps(f"hot{i}", [P, G, P]) for i in range(2)]
        ps_er = [ps(f"er{i}", [P, G, 2 * H]) for i in range(2)]
        ps_sum = ps("sum", [P, D])
        ps_den = ps("den", [P, H])
        indexed, gathered = sem("indexed"), [sem(f"gathered{q}") for q in range(Q)]
        hot_ready, hot_turned, hot_copied = sem("hot_ready"), sem("hot_turned"), sem("hot_copied")
        er_ready, logits_ready, weights_ready = sem("er_ready"), sem("logits_ready"), sem("weights_ready")
        messages_ready, summed = sem("messages_ready"), sem("summed")
        block_done, block_read, out_free = sem("block_done"), sem("block_read"), sem("out_free")
        block_out = [sem(f"block_out{i}") for i in range(2)]
        ordered, filled = sem("ordered"), sem("filled")
        block = ctx.enter_context(nc.Block())

        @block.sync
        def _(sp):
            sp.sem_inc(out_free, 2)

            def store(b, s, turn):
                sp.wait_ge(block_read, b + 1)
                sp.dma_start(sums[bass.ds(b * P, P), :], out[:, s * ROW:(s + 1) * ROW]).then_inc(block_out[s], 16)
                sp.wait_ge(block_out[s], 16 * (turn + 1))
                sp.sem_inc(out_free, 1)

            with sp.Fori(0, NT // 2) as k:
                for s in range(2):
                    store(2 * k + s, s, k)
            store(NT - 1, 0, NT // 2)

        @block.gpsimd
        def _(pool):
            pool.memset(junk[:, :], 0.0).then_inc(filled, 1)
            pool.wait_ge(filled, 1)

            def gather(g, q):
                pool.wait_ge(indexed, g + 1)
                pool.tensor_tensor(junk[:, q:q + 1], junk[:, Q:Q + 1], junk[:, Q:Q + 1], ALU.add).then_inc(filled, 1)
                for j in range(G):
                    pool.indirect_dma_start(
                        out=rows[:, q, j], out_offset=None, in_=table,
                        in_offset=bass.IndirectOffsetOnAxis(ap=index[:, q, j:j + 1], axis=0)).then_inc(gathered[q], 16)

            def one_pass(k):
                for q in range(Q):
                    gather(Q * k + q, q)

            looped(pool, None, NPASS, one_pass)
            gather(NG, 0)

        @block.vector
        def _(dve):
            link = Chain(dve, ordered)

            def hots(g, q):
                wait(dve, summed, g - Q + 1)
                for j in range(G):
                    ins = dve.tensor_scalar(hot[:, q, j], c.lane[:, :], c.step_dst[:, bass.ds(g * G + j, 1)], None, ALU.is_equal)
                ins.then_inc(hot_ready, 1)

            def logits(g, q, b, turn):
                dve.wait_ge(er_ready, g + 1)
                dve.wait_ge(gathered[q], 16 * G * (turn + 1))
                wait(dve, weights_ready, g - 1)
                link(dve.tensor_tensor(z[:, b], rows[:, q, :, D:ROW], ps_er[b][:, :, H:], ALU.add))
                link(dve.scalar_tensor_tensor(z[:, b], z[:, b], NEG_SLOPE, z[:, b], ALU.mult, ALU.max))
                link(dve.tensor_tensor(z[:, b], z[:, b], ps_er[b][:, :, 0:H], ALU.subtract))
                dve.tensor_scalar(z2[:, b], z[:, b], 0.0, None, ALU.min).then_inc(logits_ready, 1)

            def messages(g, q, b):
                dve.wait_ge(weights_ready, g + 1)
                wait(dve, summed, g - 1)
                dve.tensor_tensor(message[:, b].rearrange("p g (h f) -> p g h f", h=H),
                                  rows[:, q, :, 0:D].rearrange("p g (h f) -> p g h f", h=H),
                                  weight[:, b].unsqueeze(3).broadcast_to([P, G, H, HD]), ALU.mult).then_inc(messages_ready, 1)

            def indices(g, q):
                wait(dve, messages_ready, g - Q + 1)
                wait(dve, filled, g - Q + 2 if not isinstance(g, int) or g >= Q else 0)
                dve.tensor_scalar(index[:, q], c.step_src[:, bass.ds(g * G, G)], 0.0, None, ALU.add).then_inc(indexed, 1)

            for g in range(Q):
                indices(g, g)
            hots(0, 0)
            hots(1, 1)
            logits(0, 0, 0, 0)

            def one_pass(k):
                for q in range(Q):
                    g = Q * k + q
                    hots(g + 2, (q + 2) % Q)
                    logits(g + 1, (q + 1) % Q, (q + 1) % 2, k + (q + 1) // Q)
                    messages(g, q, q % 2)
                    indices(g + Q, q)

            looped(dve, link, NPASS, one_pass)

        @block.scalar
        def _(act):
            def copy_turned(g, b):
                act.wait_ge(hot_turned, g + 1)
                wait(act, er_ready, g - 1)
                act.copy(hotT[:, b], ps_hot[b][:, :, :]).then_inc(hot_copied, 1)

            def exp(g, b):
                act.wait_ge(logits_ready, g + 1)
                wait(act, summed, g - 1)
                act.activation(weight[:, b], z2[:, b], ACT.Exp).then_inc(weights_ready, 1)

            blocks_read = act.alloc_register("blocks_read")
            act.reg_mov(blocks_read, 0)

            def evacuate(word, s):
                with act.If(((word >> (6 + s)) & 1) == 1):
                    b = act.snap(blocks_read)
                    act.wait_ge(block_done, b + 1)
                    act.wait_ge(out_free, b + 1)
                    half = act.snap((b & 1) * ROW)
                    act.copy(out[:, bass.ds(half, D)], ps_sum[:, :])
                    act.copy(out[:, bass.ds(half + D, H)], ps_den[:, :]).then_inc(block_read, 1)
                    act.reg_add(blocks_read, blocks_read, 1)

            copy_turned(0, 0)
            copy_turned(1, 1)
            exp(0, 0)

            def one_pass(k):
                word = act.value_load(c.control[0:1, bass.ds(k, 1)], min_val=0, max_val=(1 << 22) - 1)
                for q in range(Q):
                    g = Q * k + q
                    copy_turned(g + 2, q % 2)
                    exp(g + 1, (q + 1) % 2)
                    for j in range(G):
                        evacuate(word, q * G + j)

            looped(act, None, NPASS, one_pass)

        @block.tensor
        def _(pe):
            def turn(g, q, b):
                pe.wait_ge(hot_ready, g + 1)
                wait(pe, hot_copied, g - 1)
                for j in range(G):
                    ins = pe.transpose(ps_hot[b][:, j], hot[:, q, j], c.ident[:, :])
                ins.then_inc(hot_turned, 1)

            def spread(g, b, blocks):
                pe.wait_ge(hot_copied, g + 1)
                wait(pe, logits_ready, g - 1)
                for j in range(G):
                    for part in range(3):
                        ins = pe.matmul(ps_er[b][:, j], hotT[:, b, j],
                                        c.logit3[:, part, bass.ds(blocks[j].with_bounds(min_val=0, max_val=NT - 1) * (2 * H), 2 * H)],
                                        start=part == 0, stop=part == 2)
                ins.then_inc(er_ready, 1)

            def open_block():
                pe.matmul(ps_sum[:, :], c.zeros_bf[:, 0:P], c.zeros_bf[:, :], start=True, stop=True, skip_group_check=True)
                return pe.matmul(ps_den[:, :], c.zeros_bf[:, 0:P], c.zeros_bf[:, 0:H], start=True, stop=True, skip_group_check=True)

            blocks_summed = pe.alloc_register("blocks_summed")
            pe.reg_mov(blocks_summed, 0)

            def accumulate(g, q, b, word):
                pe.wait_ge(messages_ready, g + 1)
                for j in range(G):
                    def weights_product():
                        return pe.matmul(ps_den[:, :], hot[:, q, j], weight[:, b, j], start=False, stop=True, skip_group_check=True)

                    pe.matmul(ps_sum[:, :], hot[:, q, j], message[:, b, j], start=False, stop=True, skip_group_check=True)
                    with pe.If(((word >> (6 + q * G + j)) & 1) == 1):
                        weights_product().then_inc(block_done, 1)
                        n = pe.snap(blocks_summed)
                        pe.wait_ge(block_read, n + 1)
                        ins = open_block()
                        if j == G - 1:
                            ins.then_inc(summed, 1)
                        pe.reg_add(blocks_summed, blocks_summed, 1)
                    with pe.Else():
                        ins = weights_product()
                        if j == G - 1:
                            ins.then_inc(summed, 1)

            def blocks_of(word, q):
                b, found = word & 63, []
                for s in range(q * G + G):
                    if s >= q * G:
                        b = pe.snap(b)
                        found.append(b)
                    b = b + ((word >> (6 + s)) & 1)
                return found

            def control(k):
                return pe.value_load(c.control[0:1, bass.ds(k, 1)], min_val=0, max_val=(1 << 22) - 1)

            turn(0, 0, 0)
            turn(1, 1, 1)
            open_block()
            spread(0, 0, blocks_of(control(0), 0))

            def one_pass(k):
                word = control(k)
                for q in range(Q):
                    g = Q * k + q
                    following = word if q < Q - 1 else control(k + 1)
                    spread(g + 1, (q + 1) % 2, blocks_of(following, (q + 1) % Q))
                    turn(g + 2, (q + 2) % Q, q % 2)
                    accumulate(g, q, q % 2, word)

            looped(pe, None, NPASS, one_pass)


def node_update_phase(nc, c, x, sums, x1_rows, Wr, br):
    with ExitStack() as ctx:
        sb, ps, sem = tensors(nc, ctx, "upd")
        wr = sb("wr", [P, KC, NX])
        brb = sb("brb", [P, NX])
        agg = sb("agg", [P, 2, ROW])
        xt = sb("xt", [P, 2, D])
        den = sb("den", [P, 2, H])
        rst = sb("rst", [P, 2, D])
        stats = sb("stats", [P, 2, 6])
        mv = sb("mv", [P, 2, 2])
        std = sb("std", [P, 2, 1])
        row = sb("row", [P, 2, XROW])
        xn = sb("xn", [P, 2, D])
        xT = sb("xT", [P, 2, D])
        ps_t = [ps(f"t{i}", [P, D]) for i in range(2)]
        ps_r = [ps(f"r{i}", [P, NX]) for i in range(2)]
        weights_in = sem("weights_in")
        tile_in = [sem(f"tile_in{i}") for i in range(2)]
        row_out = [sem(f"row_out{i}") for i in range(2)]
        added, moments, std_ready, xn_ready = sem("added"), sem("moments"), sem("std_ready"), sem("xn_ready")
        transposed, copied, routed, routes_read, ordered = (sem("transposed"), sem("copied"), sem("routed"),
                                                            sem("routes_read"), sem("ordered"))
        block = ctx.enter_context(nc.Block())

        @block.sync
        def _(sp):
            sp.dma_start(wr[:, :, :], Wr.rearrange("(k p) n -> p k n", p=P)).then_inc(weights_in, 16)
            sp.dma_start(brb[:, :], br.rearrange("(o n) -> o n", o=1).broadcast_to([P, NX])).then_inc(weights_in, 16)

            def load(i, s, rows=P):
                wait(sp, added, i - 1)
                sp.dma_start(agg[:, s], sums[bass.ds(i * P, P), :]).then_inc(tile_in[s], 16)
                sp.dma_start(xt[0:rows, s], x[bass.ds(i * P, rows), :]).then_inc(tile_in[s], 16)

            def store(i, s):
                sp.wait_ge(xn_ready, i + 1)
                sp.dma_start(x1_rows[bass.ds(i * P, P), :], row[:, s]).then_inc(row_out[s], 16)

            load(0, 0)

            def two(k):
                load(2 * k + 1, 1)
                store(2 * k, 0)
                load(2 * k + 2, 0)
                store(2 * k + 1, 1)

            looped(sp, None, NT // 2 - 1, two)
            load(NT - 2, 1)
            store(NT - 3, 0)
            load(NT - 1, 0, NLAST)
            store(NT - 2, 1)
            store(NT - 1, 0)
            sp.wait_ge(row_out[0], 16 * (NT // 2 + 1))
            sp.wait_ge(row_out[1], 16 * (NT // 2))

        @block.vector
        def _(dve):
            link = Chain(dve, ordered)
            dve.wait_ge(weights_in, 32)

            def update(i, s, turn):
                dve.wait_ge(tile_in[s], 32 * (turn + 1))
                link(dve.tensor_scalar(den[:, s], agg[:, s, D:ROW], 1e-16, None, ALU.max))
                link(dve.reciprocal(den[:, s], den[:, s]))
                link(dve.tensor_tensor(rst[:, s].rearrange("p (h f) -> p h f", h=H),
                                       agg[:, s, 0:D].rearrange("p (h f) -> p h f", h=H),
                                       den[:, s].unsqueeze(2).broadcast_to([P, H, HD]), ALU.mult))
                wait(dve, row_out[s], 16 * turn)
                dve.tensor_tensor(row[:, s, 0:D], xt[:, s], rst[:, s], ALU.add).then_inc(added, 1)
                dve.wait_ge(added, i + 1)
                link(dve.bn_stats(stats[:, s], row[:, s, 0:D]))
                carry_wait(dve, c)
                dve.bn_aggr(mv[:, s], stats[:, s]).then_inc(moments, 1)

            def normalise(i, s):
                dve.wait_ge(std_ready, i + 1)
                dve.tensor_copy(row[:, s, D:D + 1], mv[:, s, 0:1])
                link(dve.reciprocal(row[:, s, D + 1:XROW], std[:, s]))
                wait(dve, transposed, i - 1)
                dve.tensor_scalar(xn[:, s], row[:, s, 0:D], mv[:, s, 0:1], row[:, s, D + 1:XROW],
                                  ALU.subtract, ALU.mult).then_inc(xn_ready, 1)

            def keep_routes(i, s):
                dve.wait_ge(routed, i + 1)
                dve.tensor_tensor(c.route[:, bass.ds(i * NX, NX)], ps_r[s][:, :], brb[:, :], ALU.add).then_inc(routes_read, 1)

            update(0, 0, 0)
            normalise(0, 0)

            def two(k):
                update(2 * k + 1, 1, k)
                keep_routes(2 * k, 0)
                normalise(2 * k + 1, 1)
                update(2 * k + 2, 0, k + 1)
                keep_routes(2 * k + 1, 1)
                normalise(2 * k + 2, 0)

            looped(dve, link, NT // 2, two)
            keep_routes(NT - 1, 0)

        @block.scalar
        def _(act):
            def root(i, s):
                act.wait_ge(moments, i + 1)
                act.activation(std[:, s], mv[:, s, 1:2], ACT.Sqrt, bias=c.eps[:, 0:1]).then_inc(std_ready, 1)

            def copy(i, s):
                act.wait_ge(transposed, i + 1)
                wait(act, routed, i - 1)
                act.copy(xT[:, s], ps_t[s][:, :]).then_inc(copied, 1)

            root(0, 0)
            copy(0, 0)

            def two(k):
                for s in (1, 0):
                    root(2 * k + 2 - s, s)
                    copy(2 * k + 2 - s, s)

            looped(act, None, NT // 2, two)

        @block.tensor
        def _(pe):
            def route(i, s):
                pe.wait_ge(xn_ready, i + 1)
                wait(pe, copied, i - 1)
                for k in range(KC):
                    ins = pe.transpose(ps_t[s][:, k * P:(k + 1) * P], xn[:, s, k * P:(k + 1) * P], c.ident[:, :])
                ins.then_inc(transposed, 1)
                pe.wait_ge(copied, i + 1)
                wait(pe, routes_read, i - 1)
                for k in range(KC):
                    ins = pe.matmul(ps_r[s][:, :], xT[:, s, k * P:(k + 1) * P], wr[:, k], start=k == 0, stop=k == KC - 1)
                ins.then_inc(routed, 1)

            pe.wait_ge(weights_in, 32)
            route(0, 0)

            def two(k):
                route(2 * k + 1, 1)
                route(2 * k + 2, 0)

            looped(pe, None, NT // 2, two)


def route_phase(nc, c, node_list):
    with ExitStack() as ctx:
        sb, ps, sem = tensors(nc, ctx, "rou")
        best = sb("best", [P, NT])
        score = sb("score", [P, NT, NX])
        rank8 = sb("rank8", [P, NX])
        chosen = sb("chosen", [P, NT, NX])
        beyond = sb("beyond", [P, 1])
        upto = sb("upto", [P, NT, NX])
        zeros = sb("zeros", [P, NT])
        tiles = sb("tiles", [P, NX])
        tiles_i = sb("tiles_i", [P, NX], I32)
        cum = sb("cum", [P, NX])
        base = sb("base", [P, NX])
        slot = sb("slot", [P, NT])
        slot_i = sb("slot_i", [P, NT], I32)
        expert_f = sb("expert_f", [1, FT])
        node_i = sb("node_i", [P, NT], I32)
        fill = sb("fill", [P, FT], I32)
        ps_in = ps("in", [P, NT * NX])
        ps_tot = ps("tot", [P, NT * NX])
        made, filled, ordered = sem("made"), sem("filled"), sem("ordered")
        chosen_ready, counted, slots_ready, listed, list_in = (sem("chosen_ready"), sem("counted"), sem("slots_ready"),
                                                               sem("listed"), sem("list_in"))
        block = ctx.enter_context(nc.Block())

        @block.sync
        def _(sp):
            sp.wait_ge(made, 2)
            sp.dma_start(node_list.rearrange("(p t) o -> p (t o)", p=P), fill[:, :]).then_inc(filled, 16)
            sp.wait_ge(listed, 16 * NT)
            sp.dma_start(c.nodes[:, :], node_list.rearrange("(t p) o -> p (t o)", p=P),
                         allow_slow_non_contiguous=True).then_inc(list_in, 16)
            sp.wait_ge(list_in, 16)

        @block.gpsimd
        def _(pool):
            pool.iota(node_i[:, :], pattern=[[P, NT]], base=0, channel_multiplier=1).then_inc(made, 1)
            pool.memset(fill[:, :], NT * P - 1).then_inc(made, 1)
            pool.wait_ge(made, 2)
            pool.wait_ge(filled, 16)
            pool.wait_ge(slots_ready, 1)
            for t in range(NT):
                pool.indirect_dma_start(out=node_list, out_offset=bass.IndirectOffsetOnAxis(ap=slot_i[:, t:t + 1], axis=0),
                                        in_=node_i[:, t:t + 1], in_offset=None, bounds_check=FT * P - 1,
                                        oob_is_err=False).then_inc(listed, 16)

        @block.vector
        def _(dve):
            link = Chain(dve, ordered)
            route = c.route[:, :].rearrange("p (t e) -> p t e", e=NX)
            dve.memset(zeros[:, :], 0.0)
            dve.tensor_scalar(beyond[:, :], c.part[:, :], float(NLAST), None, ALU.is_ge)
            link(dve.tensor_scalar(rank8[:, :], c.lane[:, 0:NX], -1.0, float(NX), ALU.mult, ALU.add))
            link(dve.tensor_reduce(best[:, :], route, AX_X, ALU.max))
            link(dve.tensor_tensor(score[:, :, :], route, best[:, :].unsqueeze(2).broadcast_to([P, NT, NX]), ALU.is_equal))
            ranks = rank8[:, :].unsqueeze(1).broadcast_to([P, NT, NX])
            link(dve.tensor_tensor(score[:, :, :], score[:, :, :], ranks, ALU.mult))
            link(dve.tensor_reduce(best[:, :], score[:, :, :], AX_X, ALU.max))
            link(dve.tensor_tensor(chosen[:, :, :], ranks, best[:, :].unsqueeze(2).broadcast_to([P, NT, NX]), ALU.is_equal))
            link(dve.tensor_scalar(chosen[:, NT - 1], chosen[:, NT - 1], beyond[:, 0:1], None, ALU.is_gt))
            dve.engine_nop().then_inc(chosen_ready, 1)
            dve.wait_ge(counted, 1)
            tot = ps_tot[:, :].rearrange("p (t e) -> p t e", e=NX)
            for e in range(NX):
                link(dve.tensor_tensor_scan(upto[:, :, e], tot[:, :, e], zeros[:, :], 0.0, ALU.add, ALU.add))
            link(dve.tensor_scalar(tiles[:, :], upto[:, NT - 1], float(P - 1), None, ALU.add))
            link(dve.tensor_copy(tiles_i[:, :], tiles[:, :]))
            link(dve.tensor_scalar(tiles_i[:, :], tiles_i[:, :], 7, None, ALU.arith_shift_right))
            link(dve.tensor_copy(tiles[:, :], tiles_i[:, :]))
            link(dve.tensor_tensor_scan(cum[:, :], tiles[:, :], zeros[:, 0:NX], 0.0, ALU.add, ALU.add))
            link(dve.tensor_tensor(base[:, :], cum[:, :], tiles[:, :], ALU.subtract))
            link(dve.tensor_scalar(base[:, :], base[:, :], float(P), None, ALU.mult))
            link(dve.tensor_tensor(upto[:, :, :], upto[:, :, :], tot, ALU.subtract))
            link(dve.tensor_tensor(upto[:, :, :], upto[:, :, :], ps_in[:, :].rearrange("p (t e) -> p t e", e=NX), ALU.add))
            link(dve.tensor_tensor(upto[:, :, :], upto[:, :, :], base[:, :].unsqueeze(1).broadcast_to([P, NT, NX]), ALU.add))
            link(dve.tensor_tensor(upto[:, :, :], upto[:, :, :], chosen[:, :, :], ALU.mult))
            link(dve.tensor_reduce(slot[:, :], upto[:, :, :], AX_X, ALU.add))
            link(dve.tensor_scalar(beyond[:, :], beyond[:, :], float(FAR), None, ALU.mult))
            link(dve.tensor_tensor(slot[:, NT - 1:NT], slot[:, NT - 1:NT], beyond[:, :], ALU.add))
            dve.tensor_copy(slot_i[:, :], slot[:, :]).then_inc(slots_ready, 1)
            link(dve.memset(expert_f[:, :], 0.0))
            for e in range(NX):
                link(dve.scalar_tensor_tensor(expert_f[:, :], c.count[0:1, 0:FT], cum[0:1, e:e + 1], expert_f[:, :],
                                              ALU.is_ge, ALU.add))
            link(dve.tensor_scalar(expert_f[:, :], expert_f[:, :], float(NX - 1), None, ALU.min))
            link(dve.tensor_copy(c.expert[:, :], expert_f[:, :]))

        @block.tensor
        def _(pe):
            pe.wait_ge(chosen_ready, 1)
            flat = chosen[:, :, :].rearrange("p t e -> p (t e)")
            pe.matmul(ps_in[:, :], c.upper[:, :], flat, start=True, stop=True)
            pe.matmul(ps_tot[:, :], c.ones[:, :], flat, start=True, stop=True).then_inc(counted, 1)


def ffn_phase(nc, c, x1_rows, W1, b1, W2, b2, y):
    R = 4
    HC = HID // P
    with ExitStack() as ctx:
        sb, ps, sem = tensors(nc, ctx, "ffn")
        w1 = sb("w1", [P, KC, NX * HID])
        w2 = sb("w2", [P, HC, NX * D])
        b1b = sb("b1b", [P, NX * HID])
        b2b = sb("b2b", [P, NX * D])
        rows = sb("rows", [P, R, XROW])
        xn = sb("xn", [P, 2, D])
        xT = sb("xT", [P, 2, D])
        h = sb("h", [P, 2, HID])
        hT = sb("hT", [P, 2, HID])
        yo = sb("yo", [P, 2, D])
        ps_x = [ps(f"x{i}", [P, D]) for i in range(2)]
        ps_h = ps("h", [P, 2, HID])
        ps_t = ps("t", [P, 2, HID])
        ps_y = [ps(f"y{i}", [P, D]) for i in range(2)]
        w_in = sem("w_in")
        gathered = [sem(f"gathered{i}") for i in range(R)]
        y_out = [sem(f"y_out{i}") for i in range(2)]
        xn_ready, x_turned, xT_ready, h_done, h_ready = sem("xn_ready"), sem("x_turned"), sem("xT_ready"), sem("h_done"), sem("h_ready")
        h_turned, hT_ready, y_done, y_ready, ordered = sem("h_turned"), sem("hT_ready"), sem("y_done"), sem("y_ready"), sem("ordered")
        block = ctx.enter_context(nc.Block())

        def passes(eng, chain, body):
            looped(eng, chain, FT // R - 1, body)
            body(FT // R - 1)

        @block.sync
        def _(sp):
            sp.dma_start(b1b[:, :], b1.rearrange("(o e) n -> o (e n)", o=1).broadcast_to([P, NX * HID])).then_inc(w_in, 16)
            sp.dma_start(b2b[:, :], b2.rearrange("(o e) n -> o (e n)", o=1).broadcast_to([P, NX * D])).then_inc(w_in, 16)
            for e in range(NX):
                sp.dma_start(w1[:, :, e * HID:(e + 1) * HID], W1[e].rearrange("(k p) n -> p k n", p=P)).then_inc(w_in, 16)
                sp.dma_start(w2[:, :, e * D:(e + 1) * D], W2[e].rearrange("(k p) n -> p k n", p=P)).then_inc(w_in, 16)

        @block.gpsimd
        def _(pool):
            def gather(t):
                if t >= R:
                    pool.wait_ge(y_ready, t - R + 1)
                pool.indirect_dma_start(out=rows[:, t % R], out_offset=None, in_=x1_rows,
                                        in_offset=bass.IndirectOffsetOnAxis(ap=c.nodes[:, t:t + 1], axis=0)).then_inc(gathered[t % R], 16)

            for t in range(R):
                gather(t)
            for t in range(FT):
                pool.wait_ge(y_ready, t + 1)
                pool.indirect_dma_start(out=y, out_offset=bass.IndirectOffsetOnAxis(ap=c.nodes[:, t:t + 1], axis=0),
                                        in_=yo[:, t % 2], in_offset=None, bounds_check=N - 1,
                                        oob_is_err=False).then_inc(y_out[t % 2], 16)
                if t + R < FT:
                    gather(t + R)
            pool.wait_ge(y_out[0], 16 * (FT // 2))
            pool.wait_ge(y_out[1], 16 * (FT // 2))

        def ahead(t, k):
            return not isinstance(k, int) or t < FT

        @block.vector
        def _(dve):
            link = Chain(dve, ordered)

            def normalise(t, r, turn):
                dve.wait_ge(gathered[r], 16 * (turn + 1))
                wait(dve, x_turned, t - 1)
                dve.tensor_scalar(xn[:, r % 2], rows[:, r, 0:D], rows[:, r, D:D + 1], rows[:, r, D + 1:XROW],
                                  ALU.subtract, ALU.mult).then_inc(xn_ready, 1)

            def hidden(t, s, e):
                dve.wait_ge(h_done, t + 1)
                wait(dve, h_turned, t - 1)
                dve.tensor_tensor(h[:, s], ps_h[:, s], b1b[:, bass.ds(e * HID, HID)], ALU.add).then_inc(h_ready, 1)

            def result(t, r, e, turn):
                s = r % 2
                dve.wait_ge(y_done, t + 1)
                wait(dve, y_out[s], 16 * turn)
                link(dve.tensor_tensor(yo[:, s], ps_y[s][:, :], b2b[:, bass.ds(e * D, D)], ALU.add))
                dve.tensor_tensor(yo[:, s], yo[:, s], rows[:, r, 0:D], ALU.add).then_inc(y_ready, 1)

            def expert(t):
                return dve.value_load(c.expert[0:1, bass.ds(t, 1)], min_val=0, max_val=NX - 1)

            dve.wait_ge(w_in, 16 * (2 + 2 * NX))
            for t in range(3):
                normalise(t, t, 0)
            hidden(0, 0, expert(0))

            def one_pass(k):
                es = {}
                for r in range(R):
                    t = R * k + r
                    if ahead(t + 3, k):
                        normalise(t + 3, (r + 3) % R, k + (r + 3) // R)
                    if r == 0:
                        es[0] = expert(t)
                    if ahead(t + 1, k):
                        es[r + 1] = expert(t + 1)
                        hidden(t + 1, (r + 1) % 2, es[r + 1])
                    result(t, r, es[r], 2 * k + r // 2)

            if True:
                start = link.made
                one_pass(0)
                per, base = link.made - start, link.n
                with dve.Fori(1, FT // R - 1) as k:
                    link.n = base + (k - 1) * per
                    one_pass(k)
                link.n = base + (FT // R - 2) * per
                one_pass(FT // R - 1)

        @block.scalar
        def _(act):
            def copy(t, s):
                act.wait_ge(x_turned, t + 1)
                wait(act, h_done, t - 1)
                act.copy(xT[:, s], ps_x[s][:, :]).then_inc(xT_ready, 1)

            def relu(t, s):
                act.wait_ge(h_turned, t + 1)
                wait(act, y_done, t - 1)
                act.activation(hT[:, s], ps_t[:, s], ACT.Relu).then_inc(hT_ready, 1)

            copy(0, 0)
            copy(1, 1)

            def one_pass(k):
                for r in range(R):
                    t = R * k + r
                    relu(t, r % 2)
                    if ahead(t + 2, k):
                        copy(t + 2, r % 2)

            passes(act, None, one_pass)

        @block.tensor
        def _(pe):
            def turn_x(t, s):
                pe.wait_ge(xn_ready, t + 1)
                wait(pe, xT_ready, t - 1)
                for k in range(KC):
                    ins = pe.transpose(ps_x[s][:, k * P:(k + 1) * P], xn[:, s, k * P:(k + 1) * P], c.ident[:, :])
                ins.then_inc(x_turned, 1)

            def first(t, s, e):
                pe.wait_ge(xT_ready, t + 1)
                wait(pe, h_ready, t - 1)
                for k in range(KC):
                    ins = pe.matmul(ps_h[:, s], xT[:, s, k * P:(k + 1) * P], w1[:, k, bass.ds(e * HID, HID)],
                                    start=k == 0, stop=k == KC - 1)
                ins.then_inc(h_done, 1)

            def turn_h(t, s):
                pe.wait_ge(h_ready, t + 1)
                wait(pe, hT_ready, t - 1)
                for k in range(HC):
                    ins = pe.transpose(ps_t[:, s, k * P:(k + 1) * P], h[:, s, k * P:(k + 1) * P], c.ident[:, :])
                ins.then_inc(h_turned, 1)

            def second(t, s, e):
                pe.wait_ge(hT_ready, t + 1)
                wait(pe, y_ready, t - 1)
                for k in range(HC):
                    ins = pe.matmul(ps_y[s][:, :], hT[:, s, k * P:(k + 1) * P], w2[:, k, bass.ds(e * D, D)],
                                    start=k == 0, stop=k == HC - 1)
                ins.then_inc(y_done, 1)

            def expert(t):
                return pe.value_load(c.expert[0:1, bass.ds(t, 1)], min_val=0, max_val=NX - 1)

            pe.wait_ge(w_in, 16 * (2 + 2 * NX))
            turn_x(0, 0)
            turn_x(1, 1)
            first(0, 0, expert(0))

            def one_pass(k):
                e = expert(R * k)
                for r in range(R):
                    t = R * k + r
                    turn_h(t, r % 2)
                    if ahead(t + 2, k):
                        turn_x(t + 2, r % 2)
                    following = e
                    if ahead(t + 1, k):
                        following = expert(t + 1)
                        first(t + 1, (r + 1) % 2, following)
                    second(t, r % 2, e)
                    e = following

            passes(pe, None, one_pass)


class Shared:

    def __init__(self, nc, ctx):
        sb = lambda name, shape, dt=F32: ctx.enter_context(nc.sbuf_tensor(name, shape, dt))
        self.lane_i = sb("lane_i", [P, P], I32)
        self.part_i = sb("part_i", [P, 1], I32)
        self.step_i = sb("step_i", [P, SCH], I32)
        self.count_i = sb("count_i", [P, STEPS + 1], I32)
        self.lane = sb("lane", [P, P])
        self.part = sb("part", [P, 1])
        self.step = sb("step", [P, SCH])
        self.count = sb("count", [P, STEPS + 1])
        self.ones = sb("ones", [P, P])
        self.zeros_bf = sb("zeros_bf", [P, D], BF16)
        self.junk = sb("junk", [1, 2])
        self.eps = sb("eps", [P, 1])
        self.ident = sb("ident", [P, P])
        self.upper = sb("upper", [P, P])
        self.logit = sb("logit", [P, NT * 2 * H])
        self.logit3 = sb("logit3", [P, 3, NT * 2 * H], BF16)
        self.step_src = sb("step_src", [P, SCH * P], I32)
        self.step_dst = sb("step_dst", [P, SCH * P])
        self.control = sb("control", [1, NPASS + 1], I32)
        self.route = sb("route", [P, NT * NX])
        self.nodes = sb("nodes", [P, FT], I32)
        self.expert = sb("expert", [1, FT], I32)


def gnn_ffn(nc, x, src, dst, W_src, b_src, W_dst, b_dst, W_val, b_val, attn_l, attn_r, Wr, br, W1, b1, W2, b2, y):
    table = nc.dram_tensor("node_table", (NT * P, ROW), F32).ap()
    src_pad = nc.dram_tensor("src_pad", (EPAD,), I32).ap()
    dst_pad = nc.dram_tensor("dst_pad", (EPAD,), I32).ap()
    sums = nc.dram_tensor("sums", (NT * P, ROW), F32).ap()
    x1_rows = nc.dram_tensor("x1_rows", (NT * P, XROW), F32).ap()
    node_list = nc.dram_tensor("node_list", (FT * P, 1), I32).ap()
    with ExitStack() as ctx:
        c = Shared(nc, ctx)
        constants(nc, c)
        node_phase(nc, c, x, W_src, b_src, W_dst, b_dst, W_val, b_val, attn_l, attn_r, table)
        edge_phase(nc, c, src, dst, src_pad, dst_pad)
        message_phase(nc, c, table, sums)
        node_update_phase(nc, c, x, sums, x1_rows, Wr, br)
        route_phase(nc, c, node_list)
        ffn_phase(nc, c, x1_rows, W1, b1, W2, b2, y)


_INS = ["x", "src", "dst"] + ["L0_gnn_" + n for n in ("W_src", "b_src", "W_dst", "b_dst", "W_val", "b_val", "attn_l", "attn_r")] \
    + ["L0_ffn_" + n for n in ("Wr", "br", "W1", "b1", "W2", "b2")]


def kernel(**inputs):
    import numpy as np
    import concourse.bacc as bacc
    from concourse.bass_utils import run_bass_kernel_spmd

    nc = bacc.Bacc("TRN2", target_bir_lowering=False, num_devices=1)
    arrays, args = {}, []
    for name in _INS:
        a = np.ascontiguousarray(inputs[name])
        arrays[f"in_{name}"] = a
        args.append(nc.dram_tensor(f"in_{name}", a.shape, mybir.dt.from_np(a.dtype), kind="ExternalInput").ap())
    out = nc.dram_tensor("out_0", (N, D), F32, kind="ExternalOutput").ap()
    gnn_ffn(nc, *args, out)
    return run_bass_kernel_spmd(nc, [arrays], core_ids=[0]).results[0]["out_0"]
```

```python
from contextlib import ExitStack

import concourse.bass as bass
from concourse import mybir

F32 = mybir.dt.float32
BF16 = mybir.dt.bfloat16
I32 = mybir.dt.int32
ALU = mybir.AluOpType
ACT = mybir.ActivationFunctionType
AX_X = mybir.AxisListType.X
RMAX = bass.bass_isa.ReduceOp.max

P = 128
N = 6250
E = 100000
D = 512
KC = D // P
H = 8
HD = D // H
NT = -(-N // P)
NLAST = N - (NT - 1) * P
ET = 784
EPAD = ET * P
STEPS = ET + NT - 1
G = 4
NG = STEPS // G
Q = 4
PASS = G * Q
NPASS = STEPS // PASS
SCH = 7
ROW = D + H
NX = 8
HID = 256
FT = NT + NX - 1
XROW = D + 2
NEG_SLOPE = 0.2
LN_EPS = 1e-5
FAR = 1 << 20
assert STEPS == NPASS * PASS and SCH * P >= STEPS + 2 * G and EPAD >= E


class Chain:

    def __init__(self, eng, sem):
        self.eng, self.sem, self.n, self.made = eng, sem, 0, 0

    def __call__(self, ins):
        ins.then_inc(self.sem, 1)
        self.n, self.made = self.n + 1, self.made + 1
        self.eng.wait_ge(self.sem, self.n)


def wait(eng, sem, value):
    if not isinstance(value, int) or value > 0:
        eng.wait_ge(sem, value)


def looped(eng, chain, first, last, body):
    per, base, before = (chain.per, chain.n, chain.made) if chain else (0, 0, 0)
    with eng.Fori(first, last) as k:
        if chain:
            chain.n = base + (k - first) * per
        body(k)
    if chain:
        assert chain.made - before == per
        chain.n = base + (last - first) * per


def below(count):
    return lambda t: not isinstance(t, int) or t < count


def tiles(eng, chain, count, ring, step, straight=1):
    def one_pass(k):
        before = chain.made if chain else 0
        for r in range(ring):
            if not isinstance(k, int) or ring * k + r < count:
                step(ring * k + r, r, k)
        if chain and isinstance(k, int):
            chain.per = chain.made - before

    last = count // ring - 1
    for k in range(straight):
        one_pass(k)
    looped(eng, chain, straight, last, one_pass)
    for k in range(last, -(-count // ring)):
        one_pass(k)


def carry_wait(dve, c):
    dve.tensor_scalar(c.junk[:, 0:1], c.junk[:, 1:2], 1.0, None, ALU.mult)


def tensors(nc, ctx, tag):
    sb = lambda name, shape, dt=F32: ctx.enter_context(nc.sbuf_tensor(f"{tag}_{name}", shape, dt))
    ps = lambda name, shape, dt=F32: ctx.enter_context(nc.psum_tensor(f"{tag}_ps_{name}", shape, dt))
    sem = lambda name: ctx.enter_context(nc.semaphore(f"{tag}_{name}"))
    return sb, ps, sem


def constants(nc, c):
    with ExitStack() as ctx:
        _, _, sem = tensors(nc, ctx, "cst")
        made, ordered = sem("made"), sem("ordered")
        block = ctx.enter_context(nc.Block())

        @block.gpsimd
        def _(pool):
            pool.iota(c.lane_i[:, :], pattern=[[1, P]], base=0, channel_multiplier=0).then_inc(made, 1)
            pool.iota(c.part_i[:, :], pattern=[[0, 1]], base=0, channel_multiplier=1).then_inc(made, 1)
            pool.iota(c.step_i[:, :], pattern=[[P, SCH]], base=0, channel_multiplier=1).then_inc(made, 1)
            pool.iota(c.count_i[:, :], pattern=[[1, STEPS + 1]], base=0, channel_multiplier=0).then_inc(made, 1)

        @block.vector
        def _(dve):
            link = Chain(dve, ordered)
            dve.wait_ge(made, 4)
            dve.tensor_copy(c.step[:, :], c.step_i[:, :])
            dve.tensor_copy(c.count[:, :], c.count_i[:, :])
            dve.memset(c.ones[:, :], 1.0)
            dve.memset(c.zeros_bf[:, :], 0.0)
            dve.memset(c.junk[:, :], 0.0)
            dve.memset(c.eps[:, :], LN_EPS)
            link(dve.tensor_copy(c.lane[:, :], c.lane_i[:, :]))
            link(dve.tensor_copy(c.part[:, :], c.part_i[:, :]))
            dve.tensor_scalar(c.ident[:, :], c.lane[:, :], c.part[:, 0:1], None, ALU.is_equal)
            dve.tensor_scalar(c.upper[:, :], c.lane[:, :], c.part[:, 0:1], None, ALU.is_gt)


def node_phase(nc, c, x, W_src, b_src, W_dst, b_dst, W_val, b_val, attn_l, attn_r, table):
    with ExitStack() as ctx:
        sb, ps, sem = tensors(nc, ctx, "nod")
        wval = sb("wval", [P, KC, D])
        wlog = sb("wlog", [P, 2, KC, D])
        attn = sb("attn", [P, 2, D])
        bias = sb("bias", [P, 3, D])
        wel = sb("wel", [P, KC, 2, H])
        bel = sb("bel", [P, 2, H])
        xt = sb("xt", [P, 4, D])
        stats = sb("stats", [P, 2, 6])
        mv = sb("mv", [P, 2, 2])
        std = sb("std", [P, 2, 1])
        rstd = sb("rstd", [P, 2, 1])
        xn = sb("xn", [P, 2, D])
        xT = sb("xT", [P, 2, D])
        row = sb("row", [P, 2, ROW])
        ps_t = [ps(f"t{i}", [P, D]) for i in range(2)]
        ps_v = [ps(f"v{i}", [P, D]) for i in range(2)]
        ps_e = [ps(f"e{i}", [P, 2 * H]) for i in range(2)]
        weights_in, weights_ready = sem("weights_in"), sem("weights_ready")
        x_in = [sem(f"x_in{i}") for i in range(4)]
        row_out = [sem(f"row_out{i}") for i in range(2)]
        moments, std_ready, xn_ready = sem("moments"), sem("std_ready"), sem("xn_ready")
        transposed, copied, projected, row_ready = sem("transposed"), sem("copied"), sem("projected"), sem("row_ready")
        ordered = sem("ordered")
        exists = below(NT)
        block = ctx.enter_context(nc.Block())

        @block.sync
        def _(sp):
            sp.dma_start(wval[:, :, :], W_val.rearrange("(k p) n -> p k n", p=P)).then_inc(weights_in, 16)
            sp.dma_start(wlog[:, 0], W_src.rearrange("(k p) n -> p k n", p=P)).then_inc(weights_in, 16)
            sp.dma_start(wlog[:, 1], W_dst.rearrange("(k p) n -> p k n", p=P)).then_inc(weights_in, 16)
            for i, a in enumerate((attn_l, attn_r)):
                sp.dma_start(attn[:, i], a.rearrange("(o h) f -> o (h f)", o=1).broadcast_to([P, D])).then_inc(weights_in, 16)
            for i, b in enumerate((b_val, b_src, b_dst)):
                sp.dma_start(bias[:, i], b.rearrange("(o n) -> o n", o=1).broadcast_to([P, D])).then_inc(weights_in, 16)

            def load(i, r):
                wait(sp, xn_ready, i - 3)
                n = NLAST if isinstance(i, int) and i == NT - 1 else P
                sp.dma_start(xt[0:n, r], x[bass.ds(i * P, n), :]).then_inc(x_in[r], 16)

            def store(i, s):
                sp.wait_ge(row_ready, i + 1)
                sp.dma_start(table[bass.ds(i * P, P), :], row[:, s]).then_inc(row_out[s], 16)

            def step(i, r, k):
                if exists(i + 3):
                    load(i + 3, (r + 3) % 4)
                store(i, r % 2)

            for i in range(3):
                load(i, i)
            tiles(sp, None, NT, 4, step)
            sp.wait_ge(row_out[0], 16 * (NT // 2 + 1))
            sp.wait_ge(row_out[1], 16 * (NT // 2))

        @block.vector
        def _(dve):
            link = Chain(dve, ordered)
            dve.wait_ge(weights_in, 16 * 8)
            for i in range(2):
                for k in range(KC):
                    link(dve.tensor_tensor(wlog[:, i, k], wlog[:, i, k], attn[:, i], ALU.mult))
                link(dve.tensor_tensor(bias[:, 1 + i], bias[:, 1 + i], attn[:, i], ALU.mult))
                for k in range(KC):
                    link(dve.tensor_reduce(wel[:, k, i], wlog[:, i, k].rearrange("p (h f) -> p h f", h=H), AX_X, ALU.add))
                ins = dve.tensor_reduce(bel[:, i], bias[:, 1 + i].rearrange("p (h f) -> p h f", h=H), AX_X, ALU.add)
                link(ins)
            dve.engine_nop().then_inc(weights_ready, 1)

            def normalise(i, r, turn):
                s = r % 2
                dve.wait_ge(x_in[r], 16 * (turn + 1))
                link(dve.bn_stats(stats[:, s], xt[:, r]))
                carry_wait(dve, c)
                dve.bn_aggr(mv[:, s], stats[:, s]).then_inc(moments, 1)
                dve.wait_ge(moments, i + 1)
                dve.wait_ge(std_ready, i + 1)
                link(dve.reciprocal(rstd[:, s], std[:, s]))
                wait(dve, transposed, i - 1)
                dve.tensor_scalar(xn[:, s], xt[:, r], mv[:, s, 0:1], rstd[:, s], ALU.subtract, ALU.mult).then_inc(xn_ready, 1)

            def evacuate(i, s, turn):
                dve.wait_ge(projected, i + 1)
                wait(dve, row_out[s], 16 * turn)
                link(dve.tensor_tensor(c.logit[:, bass.ds(i * 2 * H, 2 * H)], ps_e[s][:, :],
                                       bel[:, :, :].rearrange("p a h -> p (a h)"), ALU.add))
                dve.tensor_scalar(row[:, s, D:ROW], c.logit[:, bass.ds(i * 2 * H, H)], 1.0, None, ALU.mult)
                dve.tensor_tensor(row[:, s, 0:D], ps_v[s][:, :], bias[:, 0], ALU.add).then_inc(row_ready, 1)

            normalise(0, 0, 0)
            normalise(1, 1, 0)

            def step(i, r, k):
                if exists(i + 2):
                    normalise(i + 2, (r + 2) % 4, k + (r + 2) // 4)
                evacuate(i, r % 2, 2 * k + r // 2)

            tiles(dve, link, NT, 4, step)

        @block.scalar
        def _(act):
            def root(i, s):
                act.wait_ge(moments, i + 1)
                act.activation(std[:, s], mv[:, s, 1:2], ACT.Sqrt, bias=c.eps[:, 0:1]).then_inc(std_ready, 1)

            def copy(i, s):
                act.wait_ge(transposed, i + 1)
                wait(act, projected, i - 1)
                act.copy(xT[:, s], ps_t[s][:, :]).then_inc(copied, 1)

            root(0, 0)
            copy(0, 0)
            root(1, 1)

            def step(i, r, k):
                if exists(i + 2):
                    root(i + 2, r % 2)
                if exists(i + 1):
                    copy(i + 1, (r + 1) % 2)

            tiles(act, None, NT, 4, step)

        @block.tensor
        def _(pe):
            def transpose(i, s):
                pe.wait_ge(xn_ready, i + 1)
                wait(pe, copied, i - 1)
                for k in range(KC):
                    ins = pe.transpose(ps_t[s][:, k * P:(k + 1) * P], xn[:, s, k * P:(k + 1) * P], c.ident[:, :])
                ins.then_inc(transposed, 1)

            def project(i, s):
                pe.wait_ge(copied, i + 1)
                wait(pe, row_ready, i - 1)
                for k in range(KC):
                    pe.matmul(ps_v[s][:, :], xT[:, s, k * P:(k + 1) * P], wval[:, k], start=k == 0, stop=k == KC - 1)
                for k in range(KC):
                    ins = pe.matmul(ps_e[s][:, :], xT[:, s, k * P:(k + 1) * P],
                                    wel[:, k].rearrange("p a h -> p (a h)"), start=k == 0, stop=k == KC - 1)
                ins.then_inc(projected, 1)

            pe.wait_ge(weights_ready, 1)
            transpose(0, 0)

            def step(i, r, k):
                if exists(i + 1):
                    transpose(i + 1, (r + 1) % 2)
                project(i, r % 2)

            tiles(pe, None, NT, 4, step)


def edge_phase(nc, c, src, dst, src_pad, dst_pad):
    with ExitStack() as ctx:
        sb, ps, sem = tensors(nc, ctx, "edg")
        pad = sb("pad", [1, 2, EPAD - E], I32)
        dst_i = sb("dst_i", [P, ET], I32)
        dst_f = sb("dst_f", [P, ET])
        below = sb("below", [P, NT, 1])
        scratch = sb("scratch", [P, ET])
        last_i = sb("last_i", [P, NT], I32)
        last = sb("last", [P, NT])
        lcol_i = sb("lcol_i", [NT, 1], I32)
        lcol = sb("lcol", [NT, 1])
        block_of = sb("block_of", [P, SCH, 1])
        tile_f = sb("tile_f", [P, SCH])
        tile_i = sb("tile_i", [P, SCH], I32)
        rows_i = sb("rows_i", [P, 2, SCH, P], I32)
        rows_f = sb("rows_f", [P, 2, SCH, P])
        passed = sb("passed", [NT, STEPS + 1])
        brow = sb("brow", [1, STEPS + 1])
        bits = sb("bits", [1, 1, PASS])
        bits_i = sb("bits_i", [1, PASS], I32)
        flag = sb("flag", [1, NPASS, PASS])
        word = sb("word", [1, NPASS])
        top = sb("top", [P, 2, H])
        gtop = sb("gtop", [P, 2, H])
        z = sb("z", [P, NT, H])
        z2 = sb("z2", [P, NT, H])
        rest = sb("rest", [P, NT * 2 * H])
        ps_c = ps("c", [P, NT])
        ps_l = ps("l", [NT, 1])
        ps_b = ps("b", [1, 2, 512])
        ps_r = [ps(f"r{i}", [P, P]) for i in range(2)]
        pads_ready, padded, dst_in = sem("pads_ready"), sem("padded"), sem("dst_in")
        counted, summed, tiles_ready = sem("counted"), sem("summed"), sem("tiles_ready")
        rows_in, rows_ready = sem("rows_in"), sem("rows_ready")
        passed_ready, brow_done = sem("passed_ready"), sem("brow_done")
        turned, kept, ordered = sem("turned"), sem("kept"), sem("ordered")
        tops_ready, tops_all = sem("tops_ready"), sem("tops_all")
        block = ctx.enter_context(nc.Block())

        @block.sync
        def _(sp):
            sp.dma_start(src_pad[0:E].rearrange("(a b) -> a b", b=800), src.rearrange("(a b) -> a b", b=800)).then_inc(padded, 16)
            sp.dma_start(dst_pad[0:E].rearrange("(a b) -> a b", b=800), dst.rearrange("(a b) -> a b", b=800)).then_inc(padded, 16)
            sp.wait_ge(pads_ready, 2)
            sp.dma_start(src_pad[E:EPAD].rearrange("(o n) -> o n", o=1), pad[:, 0]).then_inc(padded, 16)
            sp.dma_start(dst_pad[E:EPAD].rearrange("(o n) -> o n", o=1), pad[:, 1]).then_inc(padded, 16)
            sp.wait_ge(padded, 64)
            sp.dma_start(dst_i[:, :], dst_pad.rearrange("(p n) -> p n", p=P)).then_inc(dst_in, 16)

        @block.gpsimd
        def _(pool):
            pool.memset(pad[:, 0], 0).then_inc(pads_ready, 1)
            pool.memset(pad[:, 1], FAR).then_inc(pads_ready, 1)
            pool.iota(bits_i[:, :], pattern=[[0, PASS]], base=0, channel_multiplier=0)
            pool.wait_ge(tops_ready, 2)
            pool.partition_all_reduce(gtop[:, :, :].rearrange("p a h -> p (a h)"),
                                      top[:, :, :].rearrange("p a h -> p (a h)"), P, RMAX).then_inc(tops_all, 1)
            pool.wait_ge(tiles_ready, 1)
            for which, pad_rows in enumerate((src_pad, dst_pad)):
                for ch in range(SCH):
                    pool.indirect_dma_start(
                        out=rows_i[:, which, ch], out_offset=None, in_=pad_rows.rearrange("(t e) -> t e", e=P),
                        in_offset=bass.IndirectOffsetOnAxis(ap=tile_i[:, ch:ch + 1], axis=0)).then_inc(rows_in, 16)
            pool.wait_ge(rows_in, 16 * 2 * SCH)

        @block.vector
        def _(dve):
            link = Chain(dve, ordered)
            el = c.logit[:, :].rearrange("p (t a h) -> p t a h", a=2, h=H)
            link(dve.tensor_reduce(top[:, 0], el[:, :, 0].rearrange("p t h -> p h t"), AX_X, ALU.max))
            link(dve.tensor_scalar(z[:, :, :], el[:, :, 0], -1.0, None, ALU.mult))
            dve.tensor_reduce(top[:, 1], z[:, :, :].rearrange("p t h -> p h t"), AX_X, ALU.max).then_inc(tops_ready, 2)
            dve.wait_ge(tops_ready, 2)
            for j in range(PASS):
                dve.memset(bits[:, :, j:j + 1], float(64 << j))
            dve.wait_ge(dst_in, 16)
            link(dve.tensor_copy(dst_f[:, :], dst_i[:, :]))
            for b in range(NT):
                end = float(P * (b + 1)) if b < NT - 1 else float(2 * FAR)
                link(dve.tensor_scalar(scratch[:, :], dst_f[:, :], end, 0.0, ALU.is_lt, ALU.add, accum_out=below[:, b]))
            dve.engine_nop().then_inc(counted, 1)
            dve.wait_ge(summed, 1)
            for n, ints, out, add in ((ps_c[:, :], last_i[:, :], last[:, :], c.count[:, 0:NT]),
                                      (ps_l[:, :], lcol_i[:, :], lcol[:, :], c.part[0:NT, 0:1])):
                link(dve.tensor_scalar(out, n, -1.0, 0.0, ALU.add, ALU.max))
                link(dve.tensor_copy(ints, out))
                link(dve.tensor_scalar(ints, ints, 7, None, ALU.arith_shift_right))
                link(dve.tensor_copy(out, ints))
                link(dve.tensor_tensor(out, out, add, ALU.add))
            for ch in range(SCH):
                link(dve.tensor_scalar(scratch[:, 0:NT], last[:, :], c.step[:, ch:ch + 1], 0.0, ALU.is_lt, ALU.add,
                                       accum_out=block_of[:, ch]))
            link(dve.tensor_tensor(tile_f[:, :], c.step[:, :], block_of[:, :, 0], ALU.subtract))
            link(dve.tensor_scalar(tile_f[:, :], tile_f[:, :], float(ET - 1), None, ALU.min))
            dve.tensor_copy(tile_i[:, :], tile_f[:, :]).then_inc(tiles_ready, 1)
            dve.tensor_scalar(passed[:, :], c.count[0:NT, :], lcol[:, 0:1], None, ALU.is_gt).then_inc(passed_ready, 1)
            dve.wait_ge(brow_done, 1)
            link(dve.tensor_copy(brow[:, 0:512], ps_b[:, 0, :]))
            link(dve.tensor_copy(brow[:, 512:STEPS + 1], ps_b[:, 1, 0:STEPS + 1 - 512]))
            flags = flag[:, :, :].rearrange("o a b -> o (a b)")
            link(dve.tensor_tensor(flags, brow[:, 1:STEPS + 1], brow[:, 0:STEPS], ALU.subtract))
            link(dve.tensor_tensor(flag[:, :, :], flag[:, :, :], bits[:, :, :].broadcast_to([1, NPASS, PASS]), ALU.mult))
            link(dve.tensor_reduce(word[:, :], flag[:, :, :], AX_X, ALU.add))
            link(dve.tensor_tensor(word[:, :], word[:, :],
                                   brow[:, 0:STEPS].rearrange("o (a b) -> o a b", b=PASS)[:, :, 0], ALU.add))
            dve.memset(c.control[:, NPASS:NPASS + 1], 0)
            link(dve.tensor_copy(c.control[:, 0:NPASS], word[:, :]))
            dve.wait_ge(tops_all, 1)
            shift = el[:, :, 0]
            link(dve.tensor_tensor(z[:, :, :], el[:, :, 1], gtop[:, 0:1].broadcast_to([P, NT, H]), ALU.add))
            link(dve.scalar_tensor_tensor(shift, z[:, :, :], NEG_SLOPE, z[:, :, :], ALU.mult, ALU.max))
            link(dve.tensor_copy(rest[:, :], c.logit[:, :]))
            for part in range(3):
                link(dve.tensor_copy(c.logit3[:, part], rest[:, :]))
                if part < 2:
                    link(dve.tensor_tensor(rest[:, :], rest[:, :], c.logit3[:, part], ALU.subtract))
            dve.wait_ge(rows_in, 16 * 2 * SCH)
            link(dve.tensor_copy(rows_f[:, :, :, :], rows_i[:, :, :, :]))
            link(dve.tensor_scalar(block_of[:, :, :], block_of[:, :, :], float(P), None, ALU.mult))
            for ch in range(SCH):
                ins = dve.tensor_scalar(rows_f[:, 1, ch], rows_f[:, 1, ch], block_of[:, ch], None, ALU.subtract)
            link(ins)
            dve.engine_nop().then_inc(rows_ready, 1)
            for n in range(2 * SCH):
                dve.wait_ge(turned, n + 1)
                out = c.step_src if n < SCH else c.step_dst
                ch = n % SCH
                dve.tensor_copy(out[:, ch * P:(ch + 1) * P], ps_r[n % 2][:, :]).then_inc(kept, 1)

        @block.tensor
        def _(pe):
            pe.wait_ge(counted, 1)
            pe.matmul(ps_c[:, :], c.ones[:, :], below[:, :, 0], start=True, stop=True)
            pe.matmul(ps_l[:, :], below[:, :, 0], c.ones[:, 0:1], start=True, stop=True).then_inc(summed, 1)
            pe.wait_ge(passed_ready, 1)
            pe.matmul(ps_b[:, 0, :], c.ones[0:NT, 0:1], passed[:, 0:512], start=True, stop=True)
            pe.matmul(ps_b[:, 1, 0:STEPS + 1 - 512], c.ones[0:NT, 0:1], passed[:, 512:STEPS + 1],
                      start=True, stop=True).then_inc(brow_done, 1)
            pe.wait_ge(rows_ready, 1)
            for n in range(2 * SCH):
                wait(pe, kept, n - 1)
                pe.transpose(ps_r[n % 2][:, :], rows_f[:, n // SCH, n % SCH], c.ident[:, :]).then_inc(turned, 1)


def message_phase(nc, c, table, sums):
    with ExitStack() as ctx:
        sb, ps, sem = tensors(nc, ctx, "msg")
        index = sb("index", [P, Q, G], I32)
        rows = sb("rows", [P, Q, G, ROW])
        hot = sb("hot", [P, Q, G, P])
        hotT = sb("hotT", [P, 2, G, P], BF16)
        z = sb("z", [P, 2, G, H])
        z2 = sb("z2", [P, 2, G, H])
        weight = sb("weight", [P, 2, G, H])
        message = sb("message", [P, 2, G, D])
        out = sb("out", [P, 2 * ROW])
        junk = sb("junk", [1, Q + 1])
        ps_hot = [ps(f"hot{i}", [P, G, P]) for i in range(2)]
        ps_er = [ps(f"er{i}", [P, G, 2 * H]) for i in range(2)]
        ps_sum = ps("sum", [P, D])
        ps_den = ps("den", [P, H])
        indexed, gathered = sem("indexed"), [sem(f"gathered{q}") for q in range(Q)]
        hot_ready, hot_turned, hot_copied = sem("hot_ready"), sem("hot_turned"), sem("hot_copied")
        er_ready, logits_ready, weights_ready = sem("er_ready"), sem("logits_ready"), sem("weights_ready")
        messages_ready, summed = sem("messages_ready"), sem("summed")
        block_done, block_read, out_free = sem("block_done"), sem("block_read"), sem("out_free")
        block_out = [sem(f"block_out{i}") for i in range(2)]
        ordered, filled = sem("ordered"), sem("filled")
        block = ctx.enter_context(nc.Block())

        @block.sync
        def _(sp):
            sp.sem_inc(out_free, 2)

            def store(b, s, turn):
                sp.wait_ge(block_read, b + 1)
                sp.dma_start(sums[bass.ds(b * P, P), :], out[:, s * ROW:(s + 1) * ROW]).then_inc(block_out[s], 16)
                sp.wait_ge(block_out[s], 16 * (turn + 1))
                sp.sem_inc(out_free, 1)

            with sp.Fori(0, NT // 2) as k:
                for s in range(2):
                    store(2 * k + s, s, k)
            store(NT - 1, 0, NT // 2)

        @block.gpsimd
        def _(pool):
            pool.memset(junk[:, :], 0.0).then_inc(filled, 1)
            pool.wait_ge(filled, 1)

            def gather(g, q):
                pool.wait_ge(indexed, g + 1)
                pool.tensor_tensor(junk[:, q:q + 1], junk[:, Q:Q + 1], junk[:, Q:Q + 1], ALU.add).then_inc(filled, 1)
                for j in range(G):
                    pool.indirect_dma_start(
                        out=rows[:, q, j], out_offset=None, in_=table,
                        in_offset=bass.IndirectOffsetOnAxis(ap=index[:, q, j:j + 1], axis=0)).then_inc(gathered[q], 16)

            def one_pass(k):
                for q in range(Q):
                    gather(Q * k + q, q)

            one_pass(0)
            looped(pool, None, 1, NPASS, one_pass)
            gather(NG, 0)

        @block.vector
        def _(dve):
            link = Chain(dve, ordered)

            def hots(g, q):
                wait(dve, summed, g - Q + 1)
                for j in range(G):
                    ins = dve.tensor_scalar(hot[:, q, j], c.lane[:, :], c.step_dst[:, bass.ds(g * G + j, 1)], None, ALU.is_equal)
                ins.then_inc(hot_ready, 1)

            def logits(g, q, b, turn):
                dve.wait_ge(er_ready, g + 1)
                dve.wait_ge(gathered[q], 16 * G * (turn + 1))
                wait(dve, weights_ready, g - 1)
                link(dve.tensor_tensor(z[:, b], rows[:, q, :, D:ROW], ps_er[b][:, :, H:], ALU.add))
                link(dve.scalar_tensor_tensor(z[:, b], z[:, b], NEG_SLOPE, z[:, b], ALU.mult, ALU.max))
                link(dve.tensor_tensor(z[:, b], z[:, b], ps_er[b][:, :, 0:H], ALU.subtract))
                dve.tensor_scalar(z2[:, b], z[:, b], 0.0, None, ALU.min).then_inc(logits_ready, 1)

            def messages(g, q, b):
                dve.wait_ge(weights_ready, g + 1)
                wait(dve, summed, g - 1)
                dve.tensor_tensor(message[:, b].rearrange("p g (h f) -> p g h f", h=H),
                                  rows[:, q, :, 0:D].rearrange("p g (h f) -> p g h f", h=H),
                                  weight[:, b].unsqueeze(3).broadcast_to([P, G, H, HD]), ALU.mult).then_inc(messages_ready, 1)

            def indices(g, q):
                wait(dve, messages_ready, g - Q + 1)
                wait(dve, filled, g - Q + 2 if not isinstance(g, int) or g >= Q else 0)
                dve.tensor_scalar(index[:, q], c.step_src[:, bass.ds(g * G, G)], 0.0, None, ALU.add).then_inc(indexed, 1)

            for g in range(Q):
                indices(g, g)
            for g in range(3):
                hots(g, g)
            logits(0, 0, 0, 0)

            def one_pass(k):
                for q in range(Q):
                    g = Q * k + q
                    messages(g, q, q % 2)
                    indices(g + Q, q)
                    logits(g + 1, (q + 1) % Q, (q + 1) % 2, k + (q + 1) // Q)
                    hots(g + 3, (q + 3) % Q)

            made = link.made
            one_pass(0)
            link.per = link.made - made
            looped(dve, link, 1, NPASS, one_pass)

        @block.scalar
        def _(act):
            def copy_turned(g, b):
                act.wait_ge(hot_turned, g + 1)
                wait(act, er_ready, g - 1)
                act.copy(hotT[:, b], ps_hot[b][:, :, :]).then_inc(hot_copied, 1)

            def exp(g, b):
                act.wait_ge(logits_ready, g + 1)
                wait(act, summed, g - 1)
                act.activation(weight[:, b], z2[:, b], ACT.Exp).then_inc(weights_ready, 1)

            blocks_read = act.alloc_register("blocks_read")
            act.reg_mov(blocks_read, 0)

            def evacuate(word, s):
                with act.If(((word >> (6 + s)) & 1) == 1):
                    b = act.snap(blocks_read)
                    act.wait_ge(block_done, b + 1)
                    act.wait_ge(out_free, b + 1)
                    half = act.snap((b & 1) * ROW)
                    act.copy(out[:, bass.ds(half, D)], ps_sum[:, :])
                    act.copy(out[:, bass.ds(half + D, H)], ps_den[:, :]).then_inc(block_read, 1)
                    act.reg_add(blocks_read, blocks_read, 1)

            for g in range(3):
                copy_turned(g, g % 2)
            exp(0, 0)

            def one_pass(k):
                word = act.value_load(c.control[0:1, bass.ds(k, 1)], min_val=0, max_val=(1 << 22) - 1)
                for q in range(Q):
                    g = Q * k + q
                    exp(g + 1, (q + 1) % 2)
                    for j in range(G):
                        evacuate(word, q * G + j)
                    copy_turned(g + 3, (q + 1) % 2)

            one_pass(0)
            looped(act, None, 1, NPASS, one_pass)

        @block.tensor
        def _(pe):
            def turn(g, q, b):
                pe.wait_ge(hot_ready, g + 1)
                wait(pe, hot_copied, g - 1)
                for j in range(G):
                    ins = pe.transpose(ps_hot[b][:, j], hot[:, q, j], c.ident[:, :])
                ins.then_inc(hot_turned, 1)

            def spread(g, b, blocks):
                pe.wait_ge(hot_copied, g + 1)
                wait(pe, logits_ready, g - 1)
                for j in range(G):
                    for part in range(3):
                        ins = pe.matmul(ps_er[b][:, j], hotT[:, b, j],
                                        c.logit3[:, part, bass.ds(blocks[j].with_bounds(min_val=0, max_val=NT - 1) * (2 * H), 2 * H)],
                                        start=part == 0, stop=part == 2)
                ins.then_inc(er_ready, 1)

            def open_block():
                pe.matmul(ps_sum[:, :], c.zeros_bf[:, 0:P], c.zeros_bf[:, :], start=True, stop=True, skip_group_check=True)
                return pe.matmul(ps_den[:, :], c.zeros_bf[:, 0:P], c.zeros_bf[:, 0:H], start=True, stop=True, skip_group_check=True)

            blocks_summed = pe.alloc_register("blocks_summed")
            pe.reg_mov(blocks_summed, 0)

            def accumulate(g, q, b, word):
                pe.wait_ge(messages_ready, g + 1)
                for j in range(G):
                    def weights_product():
                        return pe.matmul(ps_den[:, :], hot[:, q, j], weight[:, b, j], start=False, stop=True, skip_group_check=True)

                    pe.matmul(ps_sum[:, :], hot[:, q, j], message[:, b, j], start=False, stop=True, skip_group_check=True)
                    with pe.If(((word >> (6 + q * G + j)) & 1) == 1):
                        weights_product().then_inc(block_done, 1)
                        n = pe.snap(blocks_summed)
                        pe.wait_ge(block_read, n + 1)
                        ins = open_block()
                        if j == G - 1:
                            ins.then_inc(summed, 1)
                        pe.reg_add(blocks_summed, blocks_summed, 1)
                    with pe.Else():
                        ins = weights_product()
                        if j == G - 1:
                            ins.then_inc(summed, 1)

            def blocks_of(word, q):
                b, found = word & 63, []
                for s in range(q * G + G):
                    if s >= q * G:
                        b = pe.snap(b)
                        found.append(b)
                    b = b + ((word >> (6 + s)) & 1)
                return found

            def control(k):
                return pe.value_load(c.control[0:1, bass.ds(k, 1)], min_val=0, max_val=(1 << 22) - 1)

            open_block()
            for g in range(2):
                turn(g, g, g)
                spread(g, g, blocks_of(control(0), g))
            turn(2, 2, 0)

            def one_pass(k):
                word = control(k)
                for q in range(Q):
                    g = Q * k + q
                    accumulate(g, q, q % 2, word)
                    if q == Q - 2:
                        following = control(k + 1)
                    spread(g + 2, q % 2, blocks_of(word if q < Q - 2 else following, (q + 2) % Q))
                    turn(g + 3, (q + 3) % Q, (q + 1) % 2)

            one_pass(0)
            looped(pe, None, 1, NPASS, one_pass)


def node_update_phase(nc, c, x, sums, x1_rows, Wr, br):
    with ExitStack() as ctx:
        sb, ps, sem = tensors(nc, ctx, "upd")
        wr = sb("wr", [P, KC, NX])
        brb = sb("brb", [P, NX])
        agg = sb("agg", [P, 4, ROW])
        xt = sb("xt", [P, 4, D])
        den = sb("den", [P, 2, H])
        rst = sb("rst", [P, 2, D])
        stats = sb("stats", [P, 2, 6])
        mv = sb("mv", [P, 2, 2])
        std = sb("std", [P, 2, 1])
        row = sb("row", [P, 2, XROW])
        xn = sb("xn", [P, 2, D])
        xT = sb("xT", [P, 2, D])
        ps_t = [ps(f"t{i}", [P, D]) for i in range(2)]
        ps_r = [ps(f"r{i}", [P, NX]) for i in range(2)]
        weights_in = sem("weights_in")
        tile_in = [sem(f"tile_in{i}") for i in range(4)]
        row_out = [sem(f"row_out{i}") for i in range(2)]
        added, moments, std_ready, xn_ready = sem("added"), sem("moments"), sem("std_ready"), sem("xn_ready")
        transposed, copied, routed, routes_read, ordered = (sem("transposed"), sem("copied"), sem("routed"),
                                                            sem("routes_read"), sem("ordered"))
        exists = below(NT)
        block = ctx.enter_context(nc.Block())

        @block.sync
        def _(sp):
            sp.dma_start(wr[:, :, :], Wr.rearrange("(k p) n -> p k n", p=P)).then_inc(weights_in, 16)
            sp.dma_start(brb[:, :], br.rearrange("(o n) -> o n", o=1).broadcast_to([P, NX])).then_inc(weights_in, 16)

            def load(i, r):
                wait(sp, added, i - 3)
                n = NLAST if isinstance(i, int) and i == NT - 1 else P
                sp.dma_start(agg[:, r], sums[bass.ds(i * P, P), :]).then_inc(tile_in[r], 16)
                sp.dma_start(xt[0:n, r], x[bass.ds(i * P, n), :]).then_inc(tile_in[r], 16)

            def store(i, s):
                sp.wait_ge(xn_ready, i + 1)
                sp.dma_start(x1_rows[bass.ds(i * P, P), :], row[:, s]).then_inc(row_out[s], 16)

            def step(i, r, k):
                if exists(i + 3):
                    load(i + 3, (r + 3) % 4)
                store(i, r % 2)

            for i in range(3):
                load(i, i)
            tiles(sp, None, NT, 4, step)
            sp.wait_ge(row_out[0], 16 * (NT // 2 + 1))
            sp.wait_ge(row_out[1], 16 * (NT // 2))

        @block.vector
        def _(dve):
            link = Chain(dve, ordered)
            dve.wait_ge(weights_in, 32)

            def update(i, r, k):
                s, turn = r % 2, 2 * k + r // 2
                dve.wait_ge(tile_in[r], 32 * (k + 1))
                link(dve.tensor_scalar(den[:, s], agg[:, r, D:ROW], 1e-16, None, ALU.max))
                link(dve.reciprocal(den[:, s], den[:, s]))
                link(dve.tensor_tensor(rst[:, s].rearrange("p (h f) -> p h f", h=H),
                                       agg[:, r, 0:D].rearrange("p (h f) -> p h f", h=H),
                                       den[:, s].unsqueeze(2).broadcast_to([P, H, HD]), ALU.mult))
                wait(dve, row_out[s], 16 * turn)
                dve.tensor_tensor(row[:, s, 0:D], xt[:, r], rst[:, s], ALU.add).then_inc(added, 1)
                dve.wait_ge(added, i + 1)
                link(dve.bn_stats(stats[:, s], row[:, s, 0:D]))
                carry_wait(dve, c)
                dve.bn_aggr(mv[:, s], stats[:, s]).then_inc(moments, 1)

            def normalise(i, s):
                dve.wait_ge(std_ready, i + 1)
                dve.tensor_copy(row[:, s, D:D + 1], mv[:, s, 0:1])
                link(dve.reciprocal(row[:, s, D + 1:XROW], std[:, s]))
                wait(dve, transposed, i - 1)
                dve.tensor_scalar(xn[:, s], row[:, s, 0:D], mv[:, s, 0:1], row[:, s, D + 1:XROW],
                                  ALU.subtract, ALU.mult).then_inc(xn_ready, 1)

            def keep_routes(i, s):
                dve.wait_ge(routed, i + 1)
                dve.tensor_tensor(c.route[:, bass.ds(i * NX, NX)], ps_r[s][:, :], brb[:, :], ALU.add).then_inc(routes_read, 1)

            update(0, 0, 0)
            update(1, 1, 0)
            normalise(0, 0)

            def step(i, r, k):
                if exists(i + 1):
                    normalise(i + 1, (r + 1) % 2)
                if exists(i + 2):
                    update(i + 2, (r + 2) % 4, k + (r + 2) // 4)
                keep_routes(i, r % 2)

            tiles(dve, link, NT, 4, step)

        @block.scalar
        def _(act):
            def root(i, s):
                act.wait_ge(moments, i + 1)
                act.activation(std[:, s], mv[:, s, 1:2], ACT.Sqrt, bias=c.eps[:, 0:1]).then_inc(std_ready, 1)

            def copy(i, s):
                act.wait_ge(transposed, i + 1)
                wait(act, routed, i - 1)
                act.copy(xT[:, s], ps_t[s][:, :]).then_inc(copied, 1)

            root(0, 0)
            root(1, 1)
            copy(0, 0)

            def step(i, r, k):
                if exists(i + 2):
                    root(i + 2, r % 2)
                if exists(i + 1):
                    copy(i + 1, (r + 1) % 2)

            tiles(act, None, NT, 4, step)

        @block.tensor
        def _(pe):
            def transpose(i, s):
                pe.wait_ge(xn_ready, i + 1)
                wait(pe, copied, i - 1)
                for k in range(KC):
                    ins = pe.transpose(ps_t[s][:, k * P:(k + 1) * P], xn[:, s, k * P:(k + 1) * P], c.ident[:, :])
                ins.then_inc(transposed, 1)

            def route(i, s):
                pe.wait_ge(copied, i + 1)
                wait(pe, routes_read, i - 1)
                for k in range(KC):
                    ins = pe.matmul(ps_r[s][:, :], xT[:, s, k * P:(k + 1) * P], wr[:, k], start=k == 0, stop=k == KC - 1)
                ins.then_inc(routed, 1)

            pe.wait_ge(weights_in, 32)
            transpose(0, 0)

            def step(i, r, k):
                if exists(i + 1):
                    transpose(i + 1, (r + 1) % 2)
                route(i, r % 2)

            tiles(pe, None, NT, 4, step)


def route_phase(nc, c):
    with ExitStack() as ctx:
        sb, ps, sem = tensors(nc, ctx, "rou")
        best = sb("best", [P, NT])
        score = sb("score", [P, NT, NX])
        rank8 = sb("rank8", [P, NX])
        chosen = sb("chosen", [P, NT, NX])
        beyond = sb("beyond", [P, 1])
        upto = sb("upto", [P, NT, NX])
        zeros = sb("zeros", [P, NT])
        tiles = sb("tiles", [P, NX])
        tiles_i = sb("tiles_i", [P, NX], I32)
        cum = sb("cum", [P, NX])
        base = sb("base", [P, NX])
        slot = sb("slot", [P, NT])
        slot_i = sb("slot_i", [P, NT], I32)
        expert_f = sb("expert_f", [1, FT])
        node_i = sb("node_i", [P, NT], I32)
        node1 = sb("node1", [P, NT])
        row_i = sb("row_i", [P, NT], I32)
        tile_of = sb("tile_of", [P, NT])
        row_of = sb("row_of", [P, NT])
        place = sb("place", [P, 2, P])
        value = sb("value", [P, 2, FT])
        listed_f = sb("listed_f", [P, 2, FT])
        ps_in = ps("in", [P, NT * NX])
        ps_tot = ps("tot", [P, NT * NX])
        ps_list = ps("list", [P, FT])
        made, ordered, chosen_ready, counted = sem("made"), sem("ordered"), sem("chosen_ready"), sem("counted")
        placed, listed = sem("placed"), sem("listed")
        block = ctx.enter_context(nc.Block())

        @block.gpsimd
        def _(pool):
            pool.iota(node_i[:, :], pattern=[[P, NT]], base=1, channel_multiplier=1).then_inc(made, 1)

        @block.vector
        def _(dve):
            link = Chain(dve, ordered)
            route = c.route[:, :].rearrange("p (t e) -> p t e", e=NX)
            dve.memset(zeros[:, :], 0.0)
            dve.tensor_scalar(beyond[:, :], c.part[:, :], float(NLAST), None, ALU.is_ge)
            link(dve.tensor_scalar(rank8[:, :], c.lane[:, 0:NX], -1.0, float(NX), ALU.mult, ALU.add))
            link(dve.tensor_reduce(best[:, :], route, AX_X, ALU.max))
            link(dve.tensor_tensor(score[:, :, :], route, best[:, :].unsqueeze(2).broadcast_to([P, NT, NX]), ALU.is_equal))
            ranks = rank8[:, :].unsqueeze(1).broadcast_to([P, NT, NX])
            link(dve.tensor_tensor(score[:, :, :], score[:, :, :], ranks, ALU.mult))
            link(dve.tensor_reduce(best[:, :], score[:, :, :], AX_X, ALU.max))
            link(dve.tensor_tensor(chosen[:, :, :], ranks, best[:, :].unsqueeze(2).broadcast_to([P, NT, NX]), ALU.is_equal))
            link(dve.tensor_scalar(chosen[:, NT - 1], chosen[:, NT - 1], beyond[:, 0:1], None, ALU.is_gt))
            dve.engine_nop().then_inc(chosen_ready, 1)
            dve.wait_ge(counted, 1)
            tot = ps_tot[:, :].rearrange("p (t e) -> p t e", e=NX)
            for e in range(NX):
                link(dve.tensor_tensor_scan(upto[:, :, e], tot[:, :, e], zeros[:, :], 0.0, ALU.add, ALU.add))
            link(dve.tensor_scalar(tiles[:, :], upto[:, NT - 1], float(P - 1), None, ALU.add))
            link(dve.tensor_copy(tiles_i[:, :], tiles[:, :]))
            link(dve.tensor_scalar(tiles_i[:, :], tiles_i[:, :], 7, None, ALU.arith_shift_right))
            link(dve.tensor_copy(tiles[:, :], tiles_i[:, :]))
            link(dve.tensor_tensor_scan(cum[:, :], tiles[:, :], zeros[:, 0:NX], 0.0, ALU.add, ALU.add))
            link(dve.tensor_tensor(base[:, :], cum[:, :], tiles[:, :], ALU.subtract))
            link(dve.tensor_scalar(base[:, :], base[:, :], float(P), None, ALU.mult))
            link(dve.tensor_tensor(upto[:, :, :], upto[:, :, :], tot, ALU.subtract))
            link(dve.tensor_tensor(upto[:, :, :], upto[:, :, :], ps_in[:, :].rearrange("p (t e) -> p t e", e=NX), ALU.add))
            link(dve.tensor_tensor(upto[:, :, :], upto[:, :, :], base[:, :].unsqueeze(1).broadcast_to([P, NT, NX]), ALU.add))
            link(dve.tensor_tensor(upto[:, :, :], upto[:, :, :], chosen[:, :, :], ALU.mult))
            link(dve.tensor_reduce(slot[:, :], upto[:, :, :], AX_X, ALU.add))
            link(dve.tensor_scalar(beyond[:, :], beyond[:, :], float(FAR), None, ALU.mult))
            link(dve.tensor_tensor(slot[:, NT - 1:NT], slot[:, NT - 1:NT], beyond[:, :], ALU.add))
            link(dve.tensor_copy(slot_i[:, :], slot[:, :]))
            link(dve.tensor_scalar(row_i[:, :], slot_i[:, :], P - 1, None, ALU.bitwise_and))
            link(dve.tensor_scalar(slot_i[:, :], slot_i[:, :], 7, None, ALU.arith_shift_right))
            dve.wait_ge(made, 1)
            dve.tensor_copy(node1[:, :], node_i[:, :])
            dve.tensor_copy(row_of[:, :], row_i[:, :])
            link(dve.tensor_copy(tile_of[:, :], slot_i[:, :]))
            for t in range(NT):
                wait(dve, listed, t - 1)
                dve.tensor_scalar(value[:, t % 2], c.count[:, 0:FT], tile_of[:, t:t + 1], node1[:, t:t + 1],
                                  ALU.is_equal, ALU.mult)
                dve.tensor_scalar(place[:, t % 2], c.lane[:, :], row_of[:, t:t + 1], None, ALU.is_equal).then_inc(placed, 1)
            link(dve.memset(expert_f[:, :], 0.0))
            for e in range(NX):
                link(dve.scalar_tensor_tensor(expert_f[:, :], c.count[0:1, 0:FT], cum[0:1, e:e + 1], expert_f[:, :],
                                              ALU.is_ge, ALU.add))
            link(dve.tensor_scalar(expert_f[:, :], expert_f[:, :], float(NX - 1), None, ALU.min))
            link(dve.tensor_copy(c.expert[:, :], expert_f[:, :]))
            dve.wait_ge(listed, NT)
            link(dve.tensor_scalar(listed_f[:, 0], ps_list[:, :], 0.0, float(NT * P), ALU.is_equal, ALU.mult))
            link(dve.scalar_tensor_tensor(listed_f[:, 1], ps_list[:, :], -1.0, listed_f[:, 0], ALU.add, ALU.add))
            link(dve.tensor_copy(c.nodes[:, :], listed_f[:, 1]))

        @block.tensor
        def _(pe):
            pe.wait_ge(chosen_ready, 1)
            flat = chosen[:, :, :].rearrange("p t e -> p (t e)")
            pe.matmul(ps_in[:, :], c.upper[:, :], flat, start=True, stop=True)
            pe.matmul(ps_tot[:, :], c.ones[:, :], flat, start=True, stop=True).then_inc(counted, 1)
            for t in range(NT):
                pe.wait_ge(placed, t + 1)
                pe.matmul(ps_list[:, :], place[:, t % 2], value[:, t % 2], start=t == 0, stop=t == NT - 1).then_inc(listed, 1)


def ffn_phase(nc, c, x1_rows, W1, b1, W2, b2, y):
    R = 8
    HC = HID // P
    with ExitStack() as ctx:
        sb, ps, sem = tensors(nc, ctx, "ffn")
        w1 = sb("w1", [P, KC, NX * HID])
        w2 = sb("w2", [P, HC, NX * D])
        b1b = sb("b1b", [P, NX * HID])
        b2b = sb("b2b", [P, NX * D])
        rows = sb("rows", [P, R, XROW])
        xn = sb("xn", [P, 2, D])
        xT = sb("xT", [P, 2, D])
        h = sb("h", [P, 2, HID])
        hT = sb("hT", [P, 2, HID])
        yo = sb("yo", [P, 2, D])
        ps_x = [ps(f"x{i}", [P, D]) for i in range(2)]
        ps_h = ps("h", [P, 2, HID])
        ps_t = ps("t", [P, 2, HID])
        ps_y = [ps(f"y{i}", [P, D]) for i in range(2)]
        w_in = sem("w_in")
        gathered = [sem(f"gathered{i}") for i in range(R)]
        y_out = [sem(f"y_out{i}") for i in range(2)]
        xn_ready, x_turned, xT_ready, h_done, h_ready = sem("xn_ready"), sem("x_turned"), sem("xT_ready"), sem("h_done"), sem("h_ready")
        h_turned, hT_ready, y_done, y_ready, ordered = sem("h_turned"), sem("hT_ready"), sem("y_done"), sem("y_ready"), sem("ordered")
        block = ctx.enter_context(nc.Block())

        exists = below(FT)

        @block.sync
        def _(sp):
            sp.dma_start(b1b[:, :], b1.rearrange("(o e) n -> o (e n)", o=1).broadcast_to([P, NX * HID])).then_inc(w_in, 16)
            sp.dma_start(b2b[:, :], b2.rearrange("(o e) n -> o (e n)", o=1).broadcast_to([P, NX * D])).then_inc(w_in, 16)
            for e in range(NX):
                sp.dma_start(w1[:, :, e * HID:(e + 1) * HID], W1[e].rearrange("(k p) n -> p k n", p=P)).then_inc(w_in, 16)
                sp.dma_start(w2[:, :, e * D:(e + 1) * D], W2[e].rearrange("(k p) n -> p k n", p=P)).then_inc(w_in, 16)

        @block.gpsimd
        def _(pool):
            def gather(t):
                if t >= R:
                    pool.wait_ge(y_ready, t - R + 1)
                pool.indirect_dma_start(out=rows[:, t % R], out_offset=None, in_=x1_rows,
                                        in_offset=bass.IndirectOffsetOnAxis(ap=c.nodes[:, t:t + 1], axis=0)).then_inc(gathered[t % R], 16)

            for t in range(R):
                gather(t)
            for t in range(FT):
                pool.wait_ge(y_ready, t + 1)
                pool.indirect_dma_start(out=y, out_offset=bass.IndirectOffsetOnAxis(ap=c.nodes[:, t:t + 1], axis=0),
                                        in_=yo[:, t % 2], in_offset=None, bounds_check=N - 1,
                                        oob_is_err=False).then_inc(y_out[t % 2], 16)
                if t + R < FT:
                    gather(t + R)
            pool.wait_ge(y_out[0], 16 * (FT // 2))
            pool.wait_ge(y_out[1], 16 * (FT // 2))

        @block.vector
        def _(dve):
            link = Chain(dve, ordered)

            def normalise(t, r, turn):
                dve.wait_ge(gathered[r], 16 * (turn + 1))
                wait(dve, x_turned, t - 1)
                dve.tensor_scalar(xn[:, r % 2], rows[:, r, 0:D], rows[:, r, D:D + 1], rows[:, r, D + 1:XROW],
                                  ALU.subtract, ALU.mult).then_inc(xn_ready, 1)

            def hidden(t, s, e):
                dve.wait_ge(h_done, t + 1)
                wait(dve, h_turned, t - 1)
                dve.tensor_tensor(h[:, s], ps_h[:, s], b1b[:, bass.ds(e * HID, HID)], ALU.add).then_inc(h_ready, 1)

            def result(t, r, e, turn):
                s = r % 2
                dve.wait_ge(y_done, t + 1)
                wait(dve, y_out[s], 16 * turn)
                link(dve.tensor_tensor(yo[:, s], ps_y[s][:, :], b2b[:, bass.ds(e * D, D)], ALU.add))
                dve.tensor_tensor(yo[:, s], yo[:, s], rows[:, r, 0:D], ALU.add).then_inc(y_ready, 1)

            def expert(t):
                return dve.value_load(c.expert[0:1, bass.ds(t, 1)], min_val=0, max_val=NX - 1)

            dve.wait_ge(w_in, 16 * (2 + 2 * NX))
            for t in range(3):
                normalise(t, t, 0)
            hidden(0, 0, expert(0))

            ahead = {}

            def step(t, r, k):
                if exists(t + 3):
                    normalise(t + 3, (r + 3) % R, k + (r + 3) // R)
                e = ahead.pop(r, None)
                if e is None:
                    e = expert(t)
                if exists(t + 1):
                    following = expert(t + 1)
                    hidden(t + 1, (r + 1) % 2, following)
                    if r < R - 1:
                        ahead[r + 1] = following
                result(t, r, e, R // 2 * k + r // 2)

            tiles(dve, link, FT, R, step)

        @block.scalar
        def _(act):
            def copy(t, s):
                act.wait_ge(x_turned, t + 1)
                wait(act, h_done, t - 1)
                act.copy(xT[:, s], ps_x[s][:, :]).then_inc(xT_ready, 1)

            def relu(t, s):
                act.wait_ge(h_turned, t + 1)
                wait(act, y_done, t - 1)
                act.activation(hT[:, s], ps_t[:, s], ACT.Relu).then_inc(hT_ready, 1)

            copy(0, 0)
            copy(1, 1)

            def step(t, r, k):
                relu(t, r % 2)
                if exists(t + 2):
                    copy(t + 2, r % 2)

            tiles(act, None, FT, R, step)

        @block.tensor
        def _(pe):
            def turn_x(t, s):
                pe.wait_ge(xn_ready, t + 1)
                wait(pe, xT_ready, t - 1)
                for k in range(KC):
                    ins = pe.transpose(ps_x[s][:, k * P:(k + 1) * P], xn[:, s, k * P:(k + 1) * P], c.ident[:, :])
                ins.then_inc(x_turned, 1)

            def first(t, s, e):
                pe.wait_ge(xT_ready, t + 1)
                wait(pe, h_ready, t - 1)
                for k in range(KC):
                    ins = pe.matmul(ps_h[:, s], xT[:, s, k * P:(k + 1) * P], w1[:, k, bass.ds(e * HID, HID)],
                                    start=k == 0, stop=k == KC - 1)
                ins.then_inc(h_done, 1)

            def turn_h(t, s):
                pe.wait_ge(h_ready, t + 1)
                wait(pe, hT_ready, t - 1)
                for k in range(HC):
                    ins = pe.transpose(ps_t[:, s, k * P:(k + 1) * P], h[:, s, k * P:(k + 1) * P], c.ident[:, :])
                ins.then_inc(h_turned, 1)

            def second(t, s, e):
                pe.wait_ge(hT_ready, t + 1)
                wait(pe, y_ready, t - 1)
                for k in range(HC):
                    ins = pe.matmul(ps_y[s][:, :], hT[:, s, k * P:(k + 1) * P], w2[:, k, bass.ds(e * D, D)],
                                    start=k == 0, stop=k == HC - 1)
                ins.then_inc(y_done, 1)

            def expert(t):
                return pe.value_load(c.expert[0:1, bass.ds(t, 1)], min_val=0, max_val=NX - 1)

            pe.wait_ge(w_in, 16 * (2 + 2 * NX))
            turn_x(0, 0)
            turn_x(1, 1)
            first(0, 0, expert(0))

            ahead = {}

            def step(t, r, k):
                turn_h(t, r % 2)
                if exists(t + 2):
                    turn_x(t + 2, r % 2)
                e = ahead.pop(r, None)
                if e is None:
                    e = expert(t)
                if exists(t + 1):
                    following = expert(t + 1)
                    first(t + 1, (r + 1) % 2, following)
                    if r < R - 1:
                        ahead[r + 1] = following
                second(t, r % 2, e)

            tiles(pe, None, FT, R, step)


class Shared:

    def __init__(self, nc, ctx):
        sb = lambda name, shape, dt=F32: ctx.enter_context(nc.sbuf_tensor(name, shape, dt))
        self.lane_i = sb("lane_i", [P, P], I32)
        self.part_i = sb("part_i", [P, 1], I32)
        self.step_i = sb("step_i", [P, SCH], I32)
        self.count_i = sb("count_i", [P, STEPS + 1], I32)
        self.lane = sb("lane", [P, P])
        self.part = sb("part", [P, 1])
        self.step = sb("step", [P, SCH])
        self.count = sb("count", [P, STEPS + 1])
        self.ones = sb("ones", [P, P])
        self.zeros_bf = sb("zeros_bf", [P, D], BF16)
        self.junk = sb("junk", [1, 2])
        self.eps = sb("eps", [P, 1])
        self.ident = sb("ident", [P, P])
        self.upper = sb("upper", [P, P])
        self.logit = sb("logit", [P, NT * 2 * H])
        self.logit3 = sb("logit3", [P, 3, NT * 2 * H], BF16)
        self.step_src = sb("step_src", [P, SCH * P], I32)
        self.step_dst = sb("step_dst", [P, SCH * P])
        self.control = sb("control", [1, NPASS + 1], I32)
        self.route = sb("route", [P, NT * NX])
        self.nodes = sb("nodes", [P, FT], I32)
        self.expert = sb("expert", [1, FT], I32)


def gnn_ffn(nc, x, src, dst, W_src, b_src, W_dst, b_dst, W_val, b_val, attn_l, attn_r, Wr, br, W1, b1, W2, b2, y):
    table = nc.dram_tensor("node_table", (NT * P, ROW), F32).ap()
    src_pad = nc.dram_tensor("src_pad", (EPAD,), I32).ap()
    dst_pad = nc.dram_tensor("dst_pad", (EPAD,), I32).ap()
    sums = nc.dram_tensor("sums", (NT * P, ROW), F32).ap()
    x1_rows = nc.dram_tensor("x1_rows", (NT * P, XROW), F32).ap()
    with ExitStack() as ctx:
        c = Shared(nc, ctx)
        constants(nc, c)
        node_phase(nc, c, x, W_src, b_src, W_dst, b_dst, W_val, b_val, attn_l, attn_r, table)
        edge_phase(nc, c, src, dst, src_pad, dst_pad)
        message_phase(nc, c, table, sums)
        node_update_phase(nc, c, x, sums, x1_rows, Wr, br)
        route_phase(nc, c)
        ffn_phase(nc, c, x1_rows, W1, b1, W2, b2, y)


_INS = ["x", "src", "dst"] + ["L0_gnn_" + n for n in ("W_src", "b_src", "W_dst", "b_dst", "W_val", "b_val", "attn_l", "attn_r")] \
    + ["L0_ffn_" + n for n in ("Wr", "br", "W1", "b1", "W2", "b2")]


def kernel(**inputs):
    import numpy as np
    import concourse.bacc as bacc
    from concourse.bass_utils import run_bass_kernel_spmd

    nc = bacc.Bacc("TRN2", target_bir_lowering=False, num_devices=1)
    arrays, args = {}, []
    for name in _INS:
        a = np.ascontiguousarray(inputs[name])
        arrays[f"in_{name}"] = a
        args.append(nc.dram_tensor(f"in_{name}", a.shape, mybir.dt.from_np(a.dtype), kind="ExternalInput").ap())
    out = nc.dram_tensor("out_0", (N, D), F32, kind="ExternalOutput").ap()
    gnn_ffn(nc, *args, out)
    return run_bass_kernel_spmd(nc, [arrays], core_ids=[0]).results[0]["out_0"]
```

```python
from contextlib import ExitStack

import concourse.bass as bass
from concourse import mybir

F32 = mybir.dt.float32
BF16 = mybir.dt.bfloat16
I32 = mybir.dt.int32
ALU = mybir.AluOpType
ACT = mybir.ActivationFunctionType
AX_X = mybir.AxisListType.X
RMAX = bass.bass_isa.ReduceOp.max

P = 128
N = 6250
E = 100000
D = 512
KC = D // P
H = 8
HD = D // H
NT = -(-N // P)
NLAST = N - (NT - 1) * P
ET = 784
EPAD = ET * P
FC = 7
STEPS = ET + NT - 1
G = 4
NG = STEPS // G
Q = 8
U = 16
WG = 4
WORD = WG * G
NWORD = STEPS // WORD
NPASS = NG // U
S = 4
SCH = 7
ROW = D + H
SUM = D + H
NX = 8
HID = 256
FT = NT + NX - 1
XROW = D + 2
NEG_SLOPE = 0.2
LN_EPS = 1e-5
PROJ = D + 2 * H
BANK = 512
SPAN = 32.0
LOWEST = 1e30
FAR = 1 << 20
assert STEPS == NWORD * WORD and NG == NPASS * U and U % Q == 0 and SCH * P >= STEPS + Q * G and EPAD >= E


class Chain:

    def __init__(self, eng, sem):
        self.eng, self.sem, self.n, self.made = eng, sem, 0, 0

    def __call__(self, ins):
        ins.then_inc(self.sem, 1)
        self.n, self.made = self.n + 1, self.made + 1
        self.eng.wait_ge(self.sem, self.n)


def wait(eng, sem, value):
    if not isinstance(value, int) or value > 0:
        eng.wait_ge(sem, value)


def looped(eng, chain, first, last, body):
    per, base, before = (chain.per, chain.n, chain.made) if chain else (0, 0, 0)
    with eng.Fori(first, last) as k:
        if chain:
            chain.n = base + (k - first) * per
        body(k)
    if chain:
        assert chain.made - before == per
        chain.n = base + (last - first) * per


def below(count):
    return lambda t: not isinstance(t, int) or t < count


def tiles(eng, chain, count, ring, step, straight=1):
    def one_pass(k):
        before = chain.made if chain else 0
        for r in range(ring):
            if not isinstance(k, int) or ring * k + r < count:
                step(ring * k + r, r, k)
        if chain and isinstance(k, int):
            chain.per = chain.made - before

    last = count // ring - 1
    for k in range(straight):
        one_pass(k)
    looped(eng, chain, straight, last, one_pass)
    for k in range(last, -(-count // ring)):
        one_pass(k)


def carry_wait(dve, c):
    dve.tensor_scalar(c.junk[:, 0:1], c.junk[:, 1:2], 1.0, None, ALU.mult)


def tensors(nc, ctx, tag):
    sb = lambda name, shape, dt=F32: ctx.enter_context(nc.sbuf_tensor(f"{tag}_{name}", shape, dt))
    ps = lambda name, shape, dt=F32: ctx.enter_context(nc.psum_tensor(f"{tag}_ps_{name}", shape, dt))
    sem = lambda name: ctx.enter_context(nc.semaphore(f"{tag}_{name}"))
    return sb, ps, sem


def constants(nc, c):
    with ExitStack() as ctx:
        _, _, sem = tensors(nc, ctx, "cst")
        made, ordered = sem("made"), sem("ordered")
        block = ctx.enter_context(nc.Block())

        @block.gpsimd
        def _(pool):
            pool.iota(c.lane_i[:, :], pattern=[[1, P]], base=0, channel_multiplier=0).then_inc(made, 1)
            pool.iota(c.part_i[:, :], pattern=[[0, 1]], base=0, channel_multiplier=1).then_inc(made, 1)
            pool.iota(c.step_i[:, :], pattern=[[P, SCH]], base=0, channel_multiplier=1).then_inc(made, 1)
            pool.iota(c.count_i[:, :], pattern=[[1, STEPS + 1]], base=0, channel_multiplier=0).then_inc(made, 1)

        @block.vector
        def _(dve):
            link = Chain(dve, ordered)
            dve.wait_ge(made, 4)
            dve.tensor_copy(c.step[:, :], c.step_i[:, :])
            dve.tensor_copy(c.count[:, :], c.count_i[:, :])
            dve.memset(c.ones[:, :], 1.0)
            dve.memset(c.ones16[:, :], 1.0)
            dve.memset(c.zeros_bf[:, :], 0.0)
            dve.memset(c.junk[:, :], 0.0)
            dve.memset(c.eps[:, :], LN_EPS)
            link(dve.tensor_copy(c.lane[:, :], c.lane_i[:, :]))
            link(dve.tensor_copy(c.part[:, :], c.part_i[:, :]))
            dve.tensor_scalar(c.ident[:, :], c.lane[:, :], c.part[:, 0:1], None, ALU.is_equal)
            dve.tensor_scalar(c.upper16[:, :], c.lane[:, :], c.part[:, 0:1], None, ALU.is_gt)


def node_phase(nc, c, w, x, table):
    with ExitStack() as ctx:
        sb, ps, sem = tensors(nc, ctx, "nod")
        xt = sb("xt", [P, 4, D])
        stats = sb("stats", [P, 2, 6])
        mv = sb("mv", [P, 2, 2])
        std = sb("std", [P, 2, 1])
        rstd = sb("rstd", [P, 2, 1])
        xn = sb("xn", [P, 2, D])
        xT = sb("xT", [P, 2, D])
        row = sb("row", [P, 2, PROJ])
        ps_t = [ps(f"t{i}", [P, D]) for i in range(2)]
        ps_v = [ps(f"v{i}", [P, 2, BANK]) for i in range(2)]
        x_in = [sem(f"x_in{i}") for i in range(4)]
        row_out = [sem(f"row_out{i}") for i in range(2)]
        moments, std_ready, xn_ready = sem("moments"), sem("std_ready"), sem("xn_ready")
        transposed, copied, projected, row_ready = sem("transposed"), sem("copied"), sem("projected"), sem("row_ready")
        ordered = sem("ordered")
        exists = below(NT)
        block = ctx.enter_context(nc.Block())

        @block.sync
        def _(sp):
            def load(i, r):
                wait(sp, xn_ready, i - 3)
                n = NLAST if isinstance(i, int) and i == NT - 1 else P
                sp.dma_start(xt[0:n, r], x[bass.ds(i * P, n), :]).then_inc(x_in[r], 16)

            def store(i, s):
                sp.wait_ge(row_ready, i + 1)
                sp.dma_start(table[bass.ds(i * P, P), :], row[:, s, 0:ROW]).then_inc(row_out[s], 16)

            def step(i, r, k):
                if exists(i + 3):
                    load(i + 3, (r + 3) % 4)
                store(i, r % 2)

            for i in range(3):
                load(i, i)
            tiles(sp, None, NT, 4, step)
            sp.wait_ge(row_out[0], 16 * (NT // 2 + 1))
            sp.wait_ge(row_out[1], 16 * (NT // 2))

        @block.vector
        def _(dve):
            link = Chain(dve, ordered)

            def normalise(i, r, turn):
                s = r % 2
                dve.wait_ge(x_in[r], 16 * (turn + 1))
                link(dve.bn_stats(stats[:, s], xt[:, r]))
                carry_wait(dve, c)
                dve.bn_aggr(mv[:, s], stats[:, s]).then_inc(moments, 1)
                dve.wait_ge(moments, i + 1)
                dve.wait_ge(std_ready, i + 1)
                link(dve.reciprocal(rstd[:, s], std[:, s]))
                wait(dve, transposed, i - 1)
                dve.tensor_scalar(xn[:, s], xt[:, r], mv[:, s, 0:1], rstd[:, s], ALU.subtract, ALU.mult).then_inc(xn_ready, 1)

            def evacuate(i, s, turn):
                dve.wait_ge(projected, i + 1)
                wait(dve, row_out[s], 16 * turn)
                link(dve.tensor_tensor(row[:, s].rearrange("p (a n) -> p a n", a=2), ps_v[s][:, :, 0:PROJ // 2],
                                       w.bias[:, :].rearrange("p (a n) -> p a n", a=2), ALU.add))
                dve.tensor_scalar(c.logit[:, bass.ds(i * 2 * H, 2 * H)], row[:, s, D:PROJ], 1.0, None,
                                  ALU.mult).then_inc(row_ready, 1)

            normalise(0, 0, 0)
            normalise(1, 1, 0)

            def step(i, r, k):
                if exists(i + 2):
                    normalise(i + 2, (r + 2) % 4, k + (r + 2) // 4)
                evacuate(i, r % 2, 2 * k + r // 2)

            tiles(dve, link, NT, 4, step)

        @block.scalar
        def _(act):
            def root(i, s):
                act.wait_ge(moments, i + 1)
                act.activation(std[:, s], mv[:, s, 1:2], ACT.Sqrt, bias=c.eps[:, 0:1]).then_inc(std_ready, 1)

            def copy(i, s):
                act.wait_ge(transposed, i + 1)
                wait(act, projected, i - 1)
                act.copy(xT[:, s], ps_t[s][:, :]).then_inc(copied, 1)

            root(0, 0)
            copy(0, 0)
            root(1, 1)

            def step(i, r, k):
                if exists(i + 2):
                    root(i + 2, r % 2)
                if exists(i + 1):
                    copy(i + 1, (r + 1) % 2)

            tiles(act, None, NT, 4, step)

        @block.tensor
        def _(pe):
            def transpose(i, s):
                pe.wait_ge(xn_ready, i + 1)
                wait(pe, copied, i - 1)
                for k in range(KC):
                    ins = pe.transpose(ps_t[s][:, k * P:(k + 1) * P], xn[:, s, k * P:(k + 1) * P], c.ident[:, :])
                ins.then_inc(transposed, 1)

            def project(i, s):
                pe.wait_ge(copied, i + 1)
                wait(pe, row_ready, i - 1)
                for half in range(2):
                    for k in range(KC):
                        ins = pe.matmul(ps_v[s][:, half, 0:PROJ // 2], xT[:, s, k * P:(k + 1) * P],
                                        w.proj[:, k, half * (PROJ // 2):(half + 1) * (PROJ // 2)], start=k == 0, stop=k == KC - 1)
                ins.then_inc(projected, 1)

            transpose(0, 0)

            def step(i, r, k):
                if exists(i + 1):
                    transpose(i + 1, (r + 1) % 2)
                project(i, r % 2)

            tiles(pe, None, NT, 4, step)


def edge_phase(nc, c, w, t, src, dst, W_src, b_src, W_dst, b_dst, W_val, b_val, attn_l, attn_r, src_pad, dst_pad):
    with ExitStack() as ctx:
        sb, ps, sem = tensors(nc, ctx, "edg")
        pad = sb("pad", [1, 2, EPAD - E], I32)
        dst_i = sb("dst_i", [ET // FC, FC, P], I32)
        firsts = sb("firsts", [ET // FC, FC])
        ends = sb("ends", [P, NT])
        starts = sb("starts", [ET // FC, FC, NT])
        scratch = sb("scratch", [P, NT])
        last = sb("last", [P, NT])
        lcol = sb("lcol", [NT, 1])
        block_of = sb("block_of", [P, SCH, 1])
        tile_f = sb("tile_f", [P, SCH])
        tile_i = sb("tile_i", [P, SCH], I32)
        passed = sb("passed", [NT, STEPS + 1])
        brow = sb("brow", [1, STEPS + 1])
        bits = sb("bits", [1, 1, WORD])
        flag = sb("flag", [1, NWORD, WORD])
        word = sb("word", [1, NWORD])
        ps_c = ps("c", [P, NT])
        ps_l = ps("l", [NT, 1])
        ps_b = ps("b", [1, 2, 512])
        pads_ready, padded, dst_in = sem("pads_ready"), sem("padded"), sem("dst_in")
        counted, summed, tiles_ready = sem("counted"), sem("summed"), sem("tiles_ready")
        passed_ready, brow_done = sem("passed_ready"), sem("brow_done")
        ordered = sem("ordered")
        weights_in, values_in = sem("weights_in"), sem("values_in")
        block = ctx.enter_context(nc.Block())

        @block.sync
        def _(sp):
            sp.dma_start(src_pad[0:E].rearrange("(a b) -> a b", b=800), src.rearrange("(a b) -> a b", b=800)).then_inc(padded, 16)
            sp.dma_start(dst_pad[0:E].rearrange("(a b) -> a b", b=800), dst.rearrange("(a b) -> a b", b=800)).then_inc(padded, 16)
            sp.wait_ge(pads_ready, 2)
            sp.dma_start(src_pad[E:EPAD].rearrange("(o n) -> o n", o=1), pad[:, 0]).then_inc(padded, 16)
            sp.dma_start(dst_pad[E:EPAD].rearrange("(o n) -> o n", o=1), pad[:, 1]).then_inc(padded, 16)
            sp.wait_ge(padded, 64)
            sp.dma_start(dst_i[:, :, :], dst_pad.rearrange("(p j e) -> p j e", j=FC, e=P)).then_inc(dst_in, 16)
            for i, a in enumerate((attn_l, attn_r)):
                sp.dma_start(w.attn[:, i], a.rearrange("(o h) f -> o (h f)", o=1).broadcast_to([P, D])).then_inc(weights_in, 16)
            for i, b in enumerate((b_src, b_dst)):
                sp.dma_start(w.blog[:, i], b.rearrange("(o n) -> o n", o=1).broadcast_to([P, D])).then_inc(weights_in, 16)
            sp.dma_start(w.wlog[:, 0], W_src.rearrange("(k p) n -> p k n", p=P)).then_inc(weights_in, 16)
            sp.dma_start(w.wlog[:, 1], W_dst.rearrange("(k p) n -> p k n", p=P)).then_inc(weights_in, 16)
            sp.dma_start(w.bias[:, 0:D], b_val.rearrange("(o n) -> o n", o=1).broadcast_to([P, D])).then_inc(values_in, 16)
            sp.dma_start(w.proj[:, :, 0:D], W_val.rearrange("(k p) n -> p k n", p=P)).then_inc(values_in, 16)

        @block.gpsimd
        def _(pool):
            pool.memset(pad[:, 0], 0).then_inc(pads_ready, 1)
            pool.memset(pad[:, 1], FAR).then_inc(pads_ready, 1)
            pool.wait_ge(tiles_ready, 1)
            for which, pad_rows in enumerate((src_pad, dst_pad)):
                for ch in range(SCH):
                    pool.indirect_dma_start(
                        out=t.rows[:, which, ch], out_offset=None, in_=pad_rows.rearrange("(t e) -> t e", e=P),
                        in_offset=bass.IndirectOffsetOnAxis(ap=tile_i[:, ch:ch + 1], axis=0)).then_inc(t.rows_in, 16)

        @block.vector
        def _(dve):
            link = Chain(dve, ordered)
            link(dve.tensor_scalar(ends[:, :], c.count[:, 0:NT], float(P), float(P), ALU.mult, ALU.add))
            link(dve.memset(ends[:, NT - 1:NT], float(2 * FAR)))
            for j in range(WORD):
                dve.memset(bits[:, :, j:j + 1], float(1 << j))
            dve.wait_ge(dst_in, 16)
            link(dve.tensor_copy(firsts[:, :], dst_i[:, :, 0]))
            for j in range(FC):
                ins = dve.tensor_scalar(starts[:, j], ends[0:ET // FC, :], firsts[:, j:j + 1], None, ALU.is_gt)
            link(ins)
            dve.engine_nop().then_inc(counted, 1)
            dve.wait_ge(summed, 1)
            for n, out, add in ((ps_c[:, :], last[:, :], c.count[:, 0:NT]), (ps_l[:, :], lcol[:, :], c.part[0:NT, 0:1])):
                link(dve.tensor_scalar(out, n, -1.0, 0.0, ALU.add, ALU.max))
                link(dve.tensor_tensor(out, out, add, ALU.add))
            for ch in range(SCH):
                link(dve.tensor_scalar(scratch[:, 0:NT], last[:, :], c.step[:, ch:ch + 1], 0.0, ALU.is_lt, ALU.add,
                                       accum_out=block_of[:, ch]))
            link(dve.tensor_tensor(tile_f[:, :], c.step[:, :], block_of[:, :, 0], ALU.subtract))
            link(dve.tensor_scalar(tile_f[:, :], tile_f[:, :], float(ET - 1), None, ALU.min))
            dve.tensor_copy(tile_i[:, :], tile_f[:, :]).then_inc(tiles_ready, 1)
            dve.tensor_scalar(t.block_start[:, :], block_of[:, :, 0], -float(P), None, ALU.mult)
            dve.tensor_scalar(passed[:, :], c.count[0:NT, :], lcol[:, 0:1], None, ALU.is_gt).then_inc(passed_ready, 1)
            dve.wait_ge(weights_in, 16 * 6)
            for i in range(2):
                for k in range(KC):
                    dve.tensor_tensor(w.wlog[:, i, k], w.wlog[:, i, k], w.attn[:, i], ALU.mult)
                ins = dve.tensor_tensor(w.blog[:, i], w.blog[:, i], w.attn[:, i], ALU.mult)
            link(ins)
            for i in range(2):
                for k in range(KC):
                    dve.tensor_reduce(w.proj[:, k, D + i * H:D + (i + 1) * H],
                                      w.wlog[:, i, k].rearrange("p (h f) -> p h f", h=H), AX_X, ALU.add)
                ins = dve.tensor_reduce(w.bias[:, D + i * H:D + (i + 1) * H],
                                        w.blog[:, i].rearrange("p (h f) -> p h f", h=H), AX_X, ALU.add)
            link(ins)
            dve.wait_ge(brow_done, 1)
            link(dve.tensor_copy(brow[:, 0:512], ps_b[:, 0, :]))
            link(dve.tensor_copy(brow[:, 512:STEPS + 1], ps_b[:, 1, 0:STEPS + 1 - 512]))
            dve.tensor_copy(c.block_of_step[:, :], brow[:, 0:STEPS])
            flags = flag[:, :, :].rearrange("o a b -> o (a b)")
            link(dve.tensor_tensor(flags, brow[:, 1:STEPS + 1], brow[:, 0:STEPS], ALU.subtract))
            link(dve.tensor_tensor(flag[:, :, :], flag[:, :, :], bits[:, :, :].broadcast_to([1, NWORD, WORD]), ALU.mult))
            link(dve.tensor_reduce(word[:, :], flag[:, :, :], AX_X, ALU.add))
            dve.memset(c.control[:, NWORD:], 0)
            link(dve.tensor_copy(c.control[:, 0:NWORD], word[:, :]))
            dve.wait_ge(values_in, 32)

        @block.tensor
        def _(pe):
            pe.wait_ge(counted, 1)
            for j in range(FC):
                pe.matmul(ps_c[:, :], c.ones[0:ET // FC, :], starts[:, j], start=j == 0, stop=j == FC - 1)
            for j in range(FC):
                ins = pe.matmul(ps_l[:, :], starts[:, j], c.ones[0:ET // FC, 0:1], start=j == 0, stop=j == FC - 1)
            ins.then_inc(summed, 1)
            pe.wait_ge(passed_ready, 1)
            pe.matmul(ps_b[:, 0, :], c.ones[0:NT, 0:1], passed[:, 0:512], start=True, stop=True)
            pe.matmul(ps_b[:, 1, 0:STEPS + 1 - 512], c.ones[0:NT, 0:1], passed[:, 512:STEPS + 1],
                      start=True, stop=True).then_inc(brow_done, 1)


def shift_phase(nc, c, t, table):
    thirds = ((0, 3), (3, 3), (6, 2))
    with ExitStack() as ctx:
        sb, ps, sem = tensors(nc, ctx, "shi")
        top = sb("top", [P, 2, H])
        gtop = sb("gtop", [P, 2, H])
        z = sb("z", [P, NT, H])
        rest = sb("rest", [P, NT * 2 * H])
        span = sb("span", [P, H])
        widest = sb("widest", [P, 1])
        wide = sb("wide", [P, 1])
        wide_i = sb("wide_i", [P, 1], I32)
        bound = sb("bound", [P, (NT + 1) * H])
        index = sb("index", [P, 1], I32)
        row = sb("row", [P, ROW])
        value = sb("value", [P, H + 1])
        diagonal = sb("diagonal", [P, H + 1, P])
        others = sb("others", [P, P])
        own = sb("own", [P, H, P])
        most = sb("most", [P, H])
        junk = sb("junk", [1, 2])
        step_rows = sb("step_rows", [P, 2, SCH, P])
        ps_w = ps("w", [P, 3 * BANK])
        ps_r = [ps(f"r{i}", [P, P]) for i in range(2)]
        rows_ready, turned, kept = sem("rows_ready"), sem("turned"), sem("kept")
        top_ready, top_all, flag_ready, ordered = sem("top_ready"), sem("top_all"), sem("flag_ready"), sem("ordered")
        filled, indexed, gathered, built, spread, general = (sem("filled"), sem("indexed"), sem("gathered"), sem("built"),
                                                             sem("spread"), sem("general"))
        block = ctx.enter_context(nc.Block())

        def is_wide(eng):
            return eng.value_load(wide_i[0:1, 0:1], min_val=0, max_val=1) == 1

        @block.gpsimd
        def _(pool):
            pool.memset(junk[:, :], 0.0).then_inc(filled, 1)
            pool.wait_ge(filled, 1)
            pool.wait_ge(top_ready, 1)
            pool.partition_all_reduce(gtop[:, :, :].rearrange("p a h -> p (a h)"),
                                      top[:, :, :].rearrange("p a h -> p (a h)"), P, RMAX).then_inc(top_all, 1)

            def gather(s):
                pool.wait_ge(indexed, s + 1)
                pool.tensor_tensor(junk[:, 0:1], junk[:, 1:2], junk[:, 1:2], ALU.add).then_inc(filled, 1)
                pool.indirect_dma_start(out=row[:, :], out_offset=None, in_=table,
                                        in_offset=bass.IndirectOffsetOnAxis(ap=index[:, 0:1], axis=0)).then_inc(gathered, 16)

            pool.wait_ge(flag_ready, 1)
            with pool.If(is_wide(pool)):
                gather(0)
                with pool.Fori(1, STEPS) as s:
                    gather(s)
            with pool.Else():
                pass

        @block.tensor
        def _(pe):
            def spread_values(s):
                pe.wait_ge(built, s + 1)
                for a, (h, n) in enumerate(thirds):
                    ins = pe.matmul(ps_w[:, a * BANK:a * BANK + 3 * P], c.ones[:, :],
                                    diagonal[:, h:h + 3].rearrange("p h e -> p (h e)"), start=True, stop=True)
                ins.then_inc(spread, 1)

            for n in range(2 * SCH):
                pe.wait_ge(rows_ready, n + 1)
                wait(pe, kept, n - 1)
                pe.transpose(ps_r[n % 2][:, :], step_rows[:, n // SCH, n % SCH], c.ident[:, :]).then_inc(turned, 1)

            pe.wait_ge(flag_ready, 1)
            with pe.If(is_wide(pe)):
                spread_values(0)
                with pe.Fori(1, STEPS) as s:
                    spread_values(s)
            with pe.Else():
                pass

        @block.scalar
        def _(act):
            act.wait_ge(t.rows_in, 16 * 2 * SCH)
            for ch in range(SCH):
                act.copy(step_rows[:, 0, ch], t.rows[:, 0, ch]).then_inc(rows_ready, 1)
            for ch in range(SCH):
                act.activation(step_rows[:, 1, ch], t.rows[:, 1, ch], ACT.Identity,
                               bias=t.block_start[:, ch:ch + 1]).then_inc(rows_ready, 1)
            for n in range(2 * SCH):
                act.wait_ge(turned, n + 1)
                out, ch = (c.step_src, c.step_dst)[n // SCH], n % SCH
                act.copy(out[:, ch * P:(ch + 1) * P], ps_r[n % 2][:, :]).then_inc(kept, 1)

        @block.vector
        def _(dve):
            link = Chain(dve, ordered)
            el = c.logit[:, :].rearrange("p (t a h) -> p t a h", a=2, h=H)
            link(dve.tensor_scalar(z[:, :, :], el[:, :, 0], -1.0, None, ALU.mult))
            dve.tensor_reduce(top[:, 0], el[:, :, 0].rearrange("p t h -> p h t"), AX_X, ALU.max)
            dve.tensor_reduce(top[:, 1], z[:, :, :].rearrange("p t h -> p h t"), AX_X, ALU.max).then_inc(top_ready, 1)
            dve.wait_ge(top_all, 1)
            dve.tensor_copy(bound[:, 0:NT * H].rearrange("p (t h) -> p t h", h=H), gtop[:, 0:1].broadcast_to([P, NT, H]))
            link(dve.tensor_tensor(span[:, :], gtop[:, 0], gtop[:, 1], ALU.add))
            link(dve.tensor_reduce(widest[:, :], span[:, :], AX_X, ALU.max))
            link(dve.tensor_scalar(wide[:, :], widest[:, :], SPAN, None, ALU.is_gt))
            dve.tensor_copy(wide_i[:, :], wide[:, :]).then_inc(flag_ready, 1)
            dve.wait_ge(flag_ready, 1)

            def own_bound(s, link):
                wait(dve, gathered, 16 * s)
                wait(dve, filled, s + 1)
                dve.tensor_scalar(index[:, :], c.step_src[:, bass.ds(s, 1)], 0.0, None, ALU.add).then_inc(indexed, 1)
                dve.wait_ge(gathered, 16 * (s + 1))
                dve.tensor_scalar(value[:, 0:H], row[:, D:ROW], 1.0, None, ALU.mult)
                link(dve.tensor_scalar(value[:, H:H + 1], c.step_dst[:, bass.ds(s, 1)], 1.0, None, ALU.mult))
                dve.tensor_tensor(diagonal[:, :, :], c.ident[:, :].unsqueeze(1).broadcast_to([P, H + 1, P]),
                                  value[:, :].unsqueeze(2).broadcast_to([P, H + 1, P]), ALU.mult).then_inc(built, 1)
                dve.wait_ge(spread, s + 1)
                at_dst = 2 * BANK + 2 * P
                link(dve.tensor_scalar(others[:, :], ps_w[:, at_dst:at_dst + P], c.part[:, 0:1], None, ALU.is_equal))
                link(dve.tensor_scalar(others[:, :], others[:, :], -1.0, LOWEST, ALU.add, ALU.mult))
                for a, (h, n) in enumerate(thirds):
                    ins = dve.tensor_tensor(own[:, h:h + n], ps_w[:, a * BANK:a * BANK + n * P].rearrange("p (h e) -> p h e", h=n),
                                            others[:, :].unsqueeze(1).broadcast_to([P, n, P]), ALU.add)
                link(ins)
                link(dve.tensor_reduce(most[:, :], own[:, :, :], AX_X, ALU.max))
                at = dve.value_load(c.block_of_step[0:1, bass.ds(s, 1)], min_val=0, max_val=NT) * H
                link(dve.tensor_tensor(bound[:, bass.ds(at, H)], bound[:, bass.ds(at, H)], most[:, :], ALU.max))

            with dve.If(is_wide(dve)):
                dve.wait_ge(kept, 2 * SCH)
                inner = Chain(dve, general)
                inner(dve.memset(bound[:, :], -LOWEST))
                made = inner.made
                own_bound(0, inner)
                inner.per = inner.made - made
                looped(dve, inner, 1, STEPS, lambda s: own_bound(s, inner))
            with dve.Else():
                pass

            shift = el[:, :, 0]
            link(dve.tensor_tensor(z[:, :, :], bound[:, 0:NT * H].rearrange("p (t h) -> p t h", h=H), el[:, :, 1], ALU.add))
            link(dve.scalar_tensor_tensor(shift, z[:, :, :], NEG_SLOPE, z[:, :, :], ALU.mult, ALU.max))
            link(dve.tensor_copy(rest[:, :], c.logit[:, :]))
            rests = rest[:, :].rearrange("p (t l) -> p t l", t=NT)
            parts = c.logit3[:, 0:NT * 6 * H].rearrange("p (t a l) -> p t a l", t=NT, a=3)
            dve.memset(c.logit3[:, NT * 6 * H:], 0.0)
            for part in range(3):
                link(dve.tensor_copy(parts[:, :, part], rests))
                if part < 2:
                    link(dve.tensor_tensor(rests, rests, parts[:, :, part], ALU.subtract))


def message_phase(nc, c, table, sums):
    with ExitStack() as ctx:
        sb, ps, sem = tensors(nc, ctx, "msg")
        index = sb("index", [P, Q, G], I32)
        rows = sb("rows", [P, Q, G, ROW])
        lane16 = sb("lane16", [P, P], BF16)
        ident16 = sb("ident16", [P, P], BF16)
        hot16 = sb("hot16", [P, Q, G, P], BF16)
        hot = sb("hot", [P, Q, G, P])
        stage = sb("stage", [P, 2, G, 3, 2 * H], BF16)
        hotT = sb("hotT", [P, 2, G, P], BF16)
        z = sb("z", [P, S, G, H])
        z2 = sb("z2", [P, S, G, H])
        weight = sb("weight", [P, S, G, H])
        message = sb("message", [P, 2, G, SUM])
        out = sb("out", [P, 2 * SUM])
        junk = sb("junk", [1, Q + 1])
        ps_hot = [ps(f"hot{i}", [P, G, P], BF16) for i in range(2)]
        ps_er = [ps(f"er{i}", [P, G, 2 * H]) for i in range(2)]
        ps_sum = ps("sum", [P, 4 * BANK])
        indexed, gathered = sem("indexed"), [sem(f"gathered{q}") for q in range(Q)]
        hot_ready, hot_turned, hot_copied = sem("hot_ready"), sem("hot_turned"), sem("hot_copied")
        er_ready, logits_ready, weights_ready = sem("er_ready"), sem("logits_ready"), sem("weights_ready")
        messages_ready, summed = sem("messages_ready"), sem("summed")
        widened, staged = sem("widened"), sem("staged")
        block_done, block_read, out_free = sem("block_done"), sem("block_read"), sem("out_free")
        block_out = [sem(f"block_out{i}") for i in range(2)]
        ordered, filled = sem("ordered"), sem("filled")
        block = ctx.enter_context(nc.Block())

        @block.sync
        def _(sp):
            sp.sem_inc(out_free, 2)

            def store(b, s, turn):
                sp.wait_ge(block_read, b + 2)
                sp.dma_start(sums[bass.ds(b * P, P), :], out[:, s * SUM:(s + 1) * SUM]).then_inc(block_out[s], 16)
                sp.wait_ge(block_out[s], 16 * (turn + 1))
                sp.sem_inc(out_free, 1)

            with sp.Fori(0, NT // 2) as k:
                for s in range(2):
                    store(2 * k + s, s, k)
            store(NT - 1, 0, NT // 2)

        @block.gpsimd
        def _(pool):
            pool.memset(junk[:, :], 0.0).then_inc(filled, 1)
            pool.wait_ge(filled, 1)

            def gather_two(g, q):
                pool.wait_ge(indexed, g + 2)
                pool.tensor_tensor(junk[:, q:q + 1], junk[:, Q:Q + 1], junk[:, Q:Q + 1], ALU.add).then_inc(filled, 1)
                for r in range(q, q + 2):
                    for j in range(G):
                        pool.indirect_dma_start(
                            out=rows[:, r, j], out_offset=None, in_=table,
                            in_offset=bass.IndirectOffsetOnAxis(ap=index[:, r, j:j + 1], axis=0)).then_inc(gathered[r], 16)

            def one_pass(k):
                for q in range(0, U, 2):
                    gather_two(U * k + q, q % Q)

            one_pass(0)
            looped(pool, None, 1, NPASS, one_pass)
            gather_two(NG, NG % Q)

        @block.vector
        def _(dve):
            link = Chain(dve, ordered)
            dve.tensor_copy(ident16[:, :], c.ident[:, :])
            link(dve.tensor_copy(lane16[:, :], c.lane[:, :]))

            def hots(g, q):
                wait(dve, summed, g - Q + 1)
                for j in range(G):
                    ins = dve.tensor_scalar(hot16[:, q, j], lane16[:, :], c.step_dst[:, bass.ds(g * G + j, 1)], None, ALU.is_equal)
                ins.then_inc(hot_ready, 1)

            def logits(g, q, turn):
                dve.wait_ge(er_ready, g + 1)
                dve.wait_ge(gathered[q], 16 * G * (turn + 1))
                wait(dve, weights_ready, g - S + 1)
                b, e = q % S, q % 2
                link(dve.tensor_tensor(z[:, b], rows[:, q, :, D:ROW], ps_er[e][:, :, H:], ALU.add))
                link(dve.scalar_tensor_tensor(z[:, b], z[:, b], NEG_SLOPE, z[:, b], ALU.mult, ALU.max))
                link(dve.tensor_tensor(z[:, b], z[:, b], ps_er[e][:, :, 0:H], ALU.subtract))
                dve.tensor_scalar(z2[:, b], z[:, b], 0.0, None, ALU.min).then_inc(logits_ready, 1)

            def messages(g, q, b):
                dve.wait_ge(weights_ready, g + 1)
                wait(dve, summed, g - 1)
                dve.tensor_scalar(message[:, b, :, D:SUM], weight[:, q % S], 1.0, None, ALU.mult)
                dve.tensor_tensor(message[:, b, :, 0:D].rearrange("p g (h f) -> p g h f", h=H),
                                  rows[:, q, :, 0:D].rearrange("p g (h f) -> p g h f", h=H),
                                  weight[:, q % S].unsqueeze(3).broadcast_to([P, G, H, HD]), ALU.mult).then_inc(messages_ready, 1)

            for g in range(6):
                hots(g, g)
            logits(0, 0, 0)
            logits(1, 1, 0)

            def one_pass(k):
                for q in range(U):
                    g = U * k + q
                    messages(g, q % Q, q % 2)
                    logits(g + 2, (q + 2) % Q, U // Q * k + (q + 2) // Q)
                    hots(g + 6, (q + 6) % Q)

            made = link.made
            one_pass(0)
            link.per = link.made - made
            looped(dve, link, 1, NPASS, one_pass)

        @block.scalar
        def _(act):
            def control(w):
                return act.value_load(c.control[0:1, bass.ds(w, 1)], min_val=0, max_val=(1 << WORD) - 1)

            def indices(g, q, half):
                wait(act, messages_ready, g - Q + 1)
                wait(act, filled, half - Q // 2 + 2 if not isinstance(g, int) or g >= Q else 0)
                act.copy(index[:, q], c.step_src[:, bass.ds(g * G, G)]).then_inc(indexed, 1)

            def widen(g, q):
                act.wait_ge(hot_ready, g + 1)
                wait(act, summed, g - Q + 1)
                act.copy(hot[:, q], hot16[:, q]).then_inc(widened, 1)

            def copy_turned(g, b):
                act.wait_ge(hot_turned, g + 1)
                wait(act, er_ready, g - 1)
                act.copy(hotT[:, b], ps_hot[b][:, :, :]).then_inc(hot_copied, 1)

            def stage_blocks(g, b, word, w):
                wait(act, er_ready, g - 1)
                for j in range(G):
                    at = act.snap(row_at).with_bounds(min_val=0, max_val=NT * 6 * H)
                    ins = act.copy(stage[:, b, j].rearrange("p a l -> p (a l)"), c.logit3[:, bass.ds(at, 6 * H)])
                    act.reg_add(row_at, row_at, ((word >> (w * G + j)) & 1) * (6 * H))
                ins.then_inc(staged, 1)

            def exp(g, b):
                act.wait_ge(logits_ready, g + 1)
                wait(act, messages_ready, g - S + 1)
                act.activation(weight[:, b], z2[:, b], ACT.Exp).then_inc(weights_ready, 1)

            blocks_read = act.alloc_register("blocks_read")
            act.reg_mov(blocks_read, 0)
            row_at = act.alloc_register("row_at")
            act.reg_mov(row_at, 0)

            def evacuate(word, w):
                with act.If(((word >> (w * G)) & (2 ** G - 1)) != 0):
                    for s in range(w * G, w * G + G):
                        with act.If(((word >> s) & 1) == 1):
                            b = act.snap(blocks_read)
                            act.wait_ge(block_done, b + 1)
                            act.wait_ge(out_free, b + 1)
                            half, bank = act.snap((b & 1) * SUM), act.snap((b & 1) * (2 * BANK))
                            act.copy(out[:, bass.ds(half, SUM)].rearrange("p (a n) -> p a n", a=2),
                                     ps_sum[:, bass.ds(bank, 2 * BANK)].rearrange("p (a n) -> p a n", a=2)[:, :, 0:SUM // 2]).then_inc(block_read, 1)
                            act.reg_add(blocks_read, blocks_read, 1)
                        with act.Else():
                            pass
                with act.Else():
                    pass

            for g in range(Q):
                indices(g, g, g // 2)
            words = [act.alloc_register(f"word{i}") for i in range(3)]
            for w in range(2):
                act.reg_mov(words[w], control(w))
            for g in range(5):
                widen(g, g)
                copy_turned(g, g % 2)
                stage_blocks(g, g % 2, act.snap(words[g // WG]), g % WG)
            exp(0, 0)
            exp(1, 1)

            def one_pass(k):
                for q in range(U):
                    g = U * k + q
                    exp(g + 2, (q + 2) % S)
                    widen(g + 5, (q + 5) % Q)
                    indices(g + Q, q % Q, U // 2 * k + (q + Q) // 2)
                    evacuate(act.snap(words[0]), q % WG)
                    copy_turned(g + 5, (q + 1) % 2)
                    last = q % WG == WG - 1
                    if last:
                        act.reg_mov(words[2], control(U // WG * k + q // WG + 2))
                    stage_blocks(g + 5, (q + 1) % 2, act.snap(words[2 if last else 1]), (q + 5) % WG)
                    if last:
                        act.reg_mov(words[0], act.snap(words[1]))
                        act.reg_mov(words[1], act.snap(words[2]))

            one_pass(0)
            looped(act, None, 1, NPASS, one_pass)

        @block.tensor
        def _(pe):
            def turn(g, q, b):
                pe.wait_ge(hot_ready, g + 1)
                wait(pe, hot_copied, g - 1)
                for j in range(G):
                    ins = pe.transpose(ps_hot[b][:, j], hot16[:, q, j], ident16[:, :])
                ins.then_inc(hot_turned, 1)

            def spread(g, b, e):
                pe.wait_ge(hot_copied, g + 1)
                pe.wait_ge(staged, g + 1)
                wait(pe, logits_ready, g - 1)
                for j in range(G):
                    for part in range(3):
                        ins = pe.matmul(ps_er[e][:, j], hotT[:, b, j], stage[:, b, j, part], start=part == 0, stop=part == 2)
                ins.then_inc(er_ready, 1)

            def open_block():
                at = pe.snap(bank).with_bounds(min_val=0, max_val=2 * BANK)
                for half in range(2):
                    ins = pe.matmul(ps_sum[:, half * BANK:][:, bass.ds(at, SUM // 2)], c.zeros_bf[:, 0:P], c.zeros_bf[:, 0:SUM // 2],
                                    start=True, stop=True, skip_group_check=True)
                return ins

            def step_products(q, j):
                at = pe.snap(bank).with_bounds(min_val=0, max_val=2 * BANK)
                for half in range(2):
                    ins = pe.matmul(ps_sum[:, half * BANK:][:, bass.ds(at, SUM // 2)], hot[:, q, j],
                                    message[:, q % 2, j, half * (SUM // 2):(half + 1) * (SUM // 2)],
                                    start=False, stop=True, skip_group_check=True)
                return ins

            blocks_summed = pe.alloc_register("blocks_summed")
            pe.reg_mov(blocks_summed, 0)
            bank = pe.alloc_register("bank")
            pe.reg_mov(bank, 0)
            pe.sem_inc(block_read, 1)

            def accumulate(g, q):
                word = pe.snap(word_now)
                ring = q % Q

                def inputs():
                    pe.wait_ge(widened, g + 1)
                    pe.wait_ge(messages_ready, g + 1)

                with pe.If(((word >> (q % WG * G)) & (2 ** G - 1)) != 0):
                    inputs()
                    for j in range(G):
                        with pe.If(((word >> (q % WG * G + j)) & 1) == 1):
                            step_products(ring, j).then_inc(block_done, 1)
                            pe.reg_add(blocks_summed, blocks_summed, 1)
                            n = pe.snap(blocks_summed)
                            pe.reg_mov(bank, (n & 1) * (2 * BANK))
                            pe.wait_ge(block_read, n)
                            ins = open_block()
                            if j == G - 1:
                                ins.then_inc(summed, 1)
                        with pe.Else():
                            ins = step_products(ring, j)
                            if j == G - 1:
                                ins.then_inc(summed, 1)
                with pe.Else():
                    inputs()
                    for j in range(G):
                        ins = step_products(ring, j)
                    ins.then_inc(summed, 1)

            def load_word(w):
                pe.reg_mov(word_now, pe.value_load(c.control[0:1, bass.ds(w, 1)], min_val=0, max_val=(1 << WORD) - 1))

            word_now = pe.alloc_register("word_now")
            load_word(0)
            open_block()
            for g in range(S):
                turn(g, g, g % 2)
                spread(g, g % 2, g % 2)
            turn(S, S, S % 2)

            def one_pass(k):
                for q in range(U):
                    g = U * k + q
                    accumulate(g, q)
                    if q % WG == WG - 1:
                        load_word(U // WG * k + q // WG + 1)
                    spread(g + S, q % 2, q % 2)
                    turn(g + S + 1, (q + S + 1) % Q, (q + S + 1) % 2)

            one_pass(0)
            looped(pe, None, 1, NPASS, one_pass)


def node_update_phase(nc, c, x, sums, x1_rows, Wr, br):
    with ExitStack() as ctx:
        sb, ps, sem = tensors(nc, ctx, "upd")
        wr = sb("wr", [P, KC, NX])
        brb = sb("brb", [P, NX])
        agg = sb("agg", [P, 4, SUM])
        xt = sb("xt", [P, 4, D])
        den = sb("den", [P, 2, H])
        rst = sb("rst", [P, 2, D])
        stats = sb("stats", [P, 2, 6])
        std = sb("std", [P, 2, 1])
        row = sb("row", [P, 4, XROW])
        xn = sb("xn", [P, 2, D])
        xT = sb("xT", [P, 2, D])
        ps_t = [ps(f"t{i}", [P, D]) for i in range(2)]
        ps_r = [ps(f"r{i}", [P, NX]) for i in range(2)]
        weights_in = sem("weights_in")
        tile_in = [sem(f"tile_in{i}") for i in range(4)]
        row_out = [sem(f"row_out{i}") for i in range(4)]
        den_ready, averaged = sem("den_ready"), sem("averaged")
        added, moments, std_ready, xn_ready = sem("added"), sem("moments"), sem("std_ready"), sem("xn_ready")
        transposed, copied, routed, routes_read, ordered = (sem("transposed"), sem("copied"), sem("routed"),
                                                            sem("routes_read"), sem("ordered"))
        exists = below(NT)
        block = ctx.enter_context(nc.Block())

        @block.sync
        def _(sp):
            sp.dma_start(wr[:, :, :], Wr.rearrange("(k p) n -> p k n", p=P)).then_inc(weights_in, 16)
            sp.dma_start(brb[:, :], br.rearrange("(o n) -> o n", o=1).broadcast_to([P, NX])).then_inc(weights_in, 16)

            def load(i, r):
                wait(sp, added, i - 3)
                n = NLAST if isinstance(i, int) and i == NT - 1 else P
                sp.dma_start(agg[:, r], sums[bass.ds(i * P, P), :]).then_inc(tile_in[r], 16)
                sp.dma_start(xt[0:n, r], x[bass.ds(i * P, n), :]).then_inc(tile_in[r], 16)

            def store(i, r):
                sp.wait_ge(xn_ready, i + 1)
                sp.dma_start(x1_rows[bass.ds(i * P, P), :], row[:, r]).then_inc(row_out[r], 16)

            def step(i, r, k):
                if exists(i + 3):
                    load(i + 3, (r + 3) % 4)
                if not isinstance(i, int) or i > 0:
                    store(i - 1, (r + 3) % 4)

            for i in range(3):
                load(i, i)
            tiles(sp, None, NT, 4, step)
            store(NT - 1, (NT - 1) % 4)
            for r in range(4):
                sp.wait_ge(row_out[r], 16 * -(-(NT - r) // 4))

        @block.gpsimd
        def _(pool):
            def add_mean(i, r, k):
                s = r % 2
                pool.wait_ge(den_ready, i + 1)
                pool.tensor_tensor(rst[:, s].rearrange("p (h f) -> p h f", h=H),
                                   agg[:, r, 0:D].rearrange("p (h f) -> p h f", h=H),
                                   den[:, s].unsqueeze(2).broadcast_to([P, H, HD]), ALU.mult).then_inc(averaged, 1)
                pool.wait_ge(averaged, i + 1)
                wait(pool, row_out[r], 16 * k)
                pool.tensor_tensor(row[:, r, 0:D], xt[:, r], rst[:, s], ALU.add).then_inc(added, 1)

            tiles(pool, None, NT, 4, add_mean)

        @block.vector
        def _(dve):
            link = Chain(dve, ordered)
            dve.wait_ge(weights_in, 32)

            def denominator(i, r, k):
                s = r % 2
                dve.wait_ge(tile_in[r], 32 * (k + 1))
                link(dve.tensor_scalar(den[:, s], agg[:, r, D:SUM], 1e-16, None, ALU.max))
                dve.reciprocal(den[:, s], den[:, s]).then_inc(den_ready, 1)

            def find_moments(i, r):
                s = r % 2
                dve.wait_ge(added, i + 1)
                link(dve.bn_stats(stats[:, s], row[:, r, 0:D]))
                carry_wait(dve, c)
                dve.bn_aggr(row[:, r, D:XROW], stats[:, s]).then_inc(moments, 1)

            def normalise(i, r):
                s = r % 2
                dve.wait_ge(std_ready, i + 1)
                link(dve.reciprocal(row[:, r, D + 1:XROW], std[:, s]))
                wait(dve, transposed, i - 1)
                dve.tensor_scalar(xn[:, s], row[:, r, 0:D], row[:, r, D:D + 1], row[:, r, D + 1:XROW],
                                  ALU.subtract, ALU.mult).then_inc(xn_ready, 1)

            def keep_routes(i, s):
                dve.wait_ge(routed, i + 1)
                dve.tensor_tensor(c.route[:, bass.ds(i * NX, NX)], ps_r[s][:, :], brb[:, :], ALU.add).then_inc(routes_read, 1)

            denominator(0, 0, 0)
            denominator(1, 1, 0)
            find_moments(0, 0)
            denominator(2, 2, 0)
            find_moments(1, 1)
            normalise(0, 0)

            def step(i, r, k):
                if exists(i + 3):
                    denominator(i + 3, (r + 3) % 4, k + (r + 3) // 4)
                if exists(i + 1):
                    normalise(i + 1, (r + 1) % 4)
                if exists(i + 2):
                    find_moments(i + 2, (r + 2) % 4)
                if not isinstance(i, int) or i > 0:
                    keep_routes(i - 1, (r + 1) % 2)

            tiles(dve, link, NT, 4, step)
            keep_routes(NT - 1, (NT - 1) % 2)

        @block.scalar
        def _(act):
            def root(i, r):
                act.wait_ge(moments, i + 1)
                act.activation(std[:, r % 2], row[:, r, D + 1:XROW], ACT.Sqrt, bias=c.eps[:, 0:1]).then_inc(std_ready, 1)

            def copy(i, s):
                act.wait_ge(transposed, i + 1)
                wait(act, routed, i - 1)
                act.copy(xT[:, s], ps_t[s][:, :]).then_inc(copied, 1)

            root(0, 0)
            root(1, 1)
            copy(0, 0)

            def step(i, r, k):
                if exists(i + 2):
                    root(i + 2, (r + 2) % 4)
                if exists(i + 1):
                    copy(i + 1, (r + 1) % 2)

            tiles(act, None, NT, 4, step)

        @block.tensor
        def _(pe):
            def transpose(i, s):
                pe.wait_ge(xn_ready, i + 1)
                wait(pe, copied, i - 1)
                for k in range(KC):
                    ins = pe.transpose(ps_t[s][:, k * P:(k + 1) * P], xn[:, s, k * P:(k + 1) * P], c.ident[:, :])
                ins.then_inc(transposed, 1)

            def route(i, s):
                pe.wait_ge(copied, i + 1)
                wait(pe, routes_read, i - 1)
                for k in range(KC):
                    ins = pe.matmul(ps_r[s][:, :], xT[:, s, k * P:(k + 1) * P], wr[:, k], start=k == 0, stop=k == KC - 1)
                ins.then_inc(routed, 1)

            pe.wait_ge(weights_in, 32)
            transpose(0, 0)

            def step(i, r, k):
                if exists(i + 1):
                    transpose(i + 1, (r + 1) % 2)
                route(i, r % 2)

            tiles(pe, None, NT, 4, step)


def route_phase(nc, c, f, W1, b1, W2, b2):
    R = 8
    with ExitStack() as ctx:
        sb, ps, sem = tensors(nc, ctx, "rou")
        best = sb("best", [P, NT])
        score = sb("score", [P, NT, NX])
        rank8 = sb("rank8", [P, NX])
        chosen = sb("chosen", [P, NT, NX], BF16)
        beyond = sb("beyond", [P, 1])
        upto = sb("upto", [P, NT, NX])
        zeros = sb("zeros", [P, NT])
        tiles = sb("tiles", [P, NX])
        tiles_i = sb("tiles_i", [P, NX], I32)
        cum = sb("cum", [P, NX])
        base = sb("base", [P, NX])
        slot = sb("slot", [P, NT])
        slot_i = sb("slot_i", [P, NT], I32)
        expert_f = sb("expert_f", [1, FT])
        lane1 = sb("lane1", [P, 1])
        row_i = sb("row_i", [P, NT], I32)
        tile_of = sb("tile_of", [P, NT])
        row_of = sb("row_of", [P, NT])
        place = sb("place", [P, R, P], BF16)
        value = sb("value", [P, R, 2, FT], BF16)
        listed_f = sb("listed_f", [P, 3, FT])
        ps_in = ps("in", [P, NT * NX])
        ps_tot = ps("tot", [P, NT * NX])
        ps_list = ps("list", [P, 2, FT])
        ordered, chosen_ready, counted = sem("ordered"), sem("chosen_ready"), sem("counted")
        rows_known, valued, listed = sem("rows_known"), sem("valued"), sem("listed")
        placed = [sem("placed_even"), sem("placed_odd")]
        block = ctx.enter_context(nc.Block())

        @block.sync
        def _(sp):
            sp.dma_start(f.b1b[:, :], b1.rearrange("(o e) n -> o (e n)", o=1).broadcast_to([P, NX * HID])).then_inc(f.loaded, 16)
            sp.dma_start(f.b2b[:, :], b2.rearrange("(o e) n -> o (e n)", o=1).broadcast_to([P, NX * D])).then_inc(f.loaded, 16)
            for e in range(NX):
                sp.dma_start(f.w1[:, :, e * HID:(e + 1) * HID], W1[e].rearrange("(k p) n -> p k n", p=P)).then_inc(f.loaded, 16)
                sp.dma_start(f.w2[:, :, e * D:(e + 1) * D], W2[e].rearrange("(k p) n -> p k n", p=P)).then_inc(f.loaded, 16)

        @block.gpsimd
        def _(pool):
            pool.wait_ge(rows_known, 1)
            for t in range(1, NT, 2):
                wait(pool, listed, t - R + 1)
                pool.tensor_scalar(place[:, t % R], c.lane[:, :], row_of[:, t:t + 1], None, ALU.is_equal).then_inc(placed[1], 1)

        @block.vector
        def _(dve):
            link = Chain(dve, ordered)
            route = c.route[:, :].rearrange("p (t e) -> p t e", e=NX)
            dve.memset(zeros[:, :], 0.0)
            dve.tensor_scalar(beyond[:, :], c.part[:, :], float(NLAST), None, ALU.is_ge)
            link(dve.tensor_scalar(rank8[:, :], c.lane[:, 0:NX], -1.0, float(NX), ALU.mult, ALU.add))
            link(dve.tensor_reduce(best[:, :], route, AX_X, ALU.max))
            link(dve.tensor_tensor(score[:, :, :], route, best[:, :].unsqueeze(2).broadcast_to([P, NT, NX]), ALU.is_equal))
            ranks = rank8[:, :].unsqueeze(1).broadcast_to([P, NT, NX])
            link(dve.tensor_tensor(score[:, :, :], score[:, :, :], ranks, ALU.mult))
            link(dve.tensor_reduce(best[:, :], score[:, :, :], AX_X, ALU.max))
            link(dve.tensor_tensor(chosen[:, :, :], ranks, best[:, :].unsqueeze(2).broadcast_to([P, NT, NX]), ALU.is_equal))
            link(dve.tensor_scalar(chosen[:, NT - 1], chosen[:, NT - 1], beyond[:, 0:1], None, ALU.is_gt))
            dve.engine_nop().then_inc(chosen_ready, 1)
            dve.wait_ge(counted, 1)
            tot = ps_tot[:, :].rearrange("p (t e) -> p t e", e=NX)
            for e in range(NX):
                link(dve.tensor_tensor_scan(upto[:, :, e], tot[:, :, e], zeros[:, :], 0.0, ALU.add, ALU.add))
            link(dve.tensor_scalar(tiles[:, :], upto[:, NT - 1], float(P - 1), None, ALU.add))
            link(dve.tensor_copy(tiles_i[:, :], tiles[:, :]))
            link(dve.tensor_scalar(tiles_i[:, :], tiles_i[:, :], 7, None, ALU.arith_shift_right))
            link(dve.tensor_copy(tiles[:, :], tiles_i[:, :]))
            link(dve.tensor_tensor_scan(cum[:, :], tiles[:, :], zeros[:, 0:NX], 0.0, ALU.add, ALU.add))
            link(dve.tensor_tensor(base[:, :], cum[:, :], tiles[:, :], ALU.subtract))
            link(dve.tensor_scalar(base[:, :], base[:, :], float(P), None, ALU.mult))
            link(dve.tensor_tensor(upto[:, :, :], upto[:, :, :], tot, ALU.subtract))
            link(dve.tensor_tensor(upto[:, :, :], upto[:, :, :], ps_in[:, :].rearrange("p (t e) -> p t e", e=NX), ALU.add))
            link(dve.tensor_tensor(upto[:, :, :], upto[:, :, :], base[:, :].unsqueeze(1).broadcast_to([P, NT, NX]), ALU.add))
            link(dve.tensor_tensor(upto[:, :, :], upto[:, :, :], chosen[:, :, :], ALU.mult))
            link(dve.tensor_reduce(slot[:, :], upto[:, :, :], AX_X, ALU.add))
            link(dve.tensor_scalar(beyond[:, :], beyond[:, :], float(FAR), None, ALU.mult))
            link(dve.tensor_tensor(slot[:, NT - 1:NT], slot[:, NT - 1:NT], beyond[:, :], ALU.add))
            link(dve.tensor_copy(slot_i[:, :], slot[:, :]))
            link(dve.tensor_scalar(row_i[:, :], slot_i[:, :], P - 1, None, ALU.bitwise_and))
            link(dve.tensor_scalar(slot_i[:, :], slot_i[:, :], 7, None, ALU.arith_shift_right))
            dve.tensor_copy(row_of[:, :], row_i[:, :]).then_inc(rows_known, 1)
            dve.tensor_scalar(lane1[:, :], c.part[:, :], 1.0, None, ALU.add)
            link(dve.tensor_copy(tile_of[:, :], slot_i[:, :]))
            for t in range(NT):
                wait(dve, listed, t - R + 1)
                dve.tensor_scalar(value[:, t % R, 0], c.count[:, 0:FT], tile_of[:, t:t + 1], lane1[:, 0:1],
                                  ALU.is_equal, ALU.mult)
                dve.tensor_scalar(value[:, t % R, 1], c.count[:, 0:FT], tile_of[:, t:t + 1], float(P * t),
                                  ALU.is_equal, ALU.mult).then_inc(valued, 1)
                if t % 2 == 0:
                    dve.tensor_scalar(place[:, t % R], c.lane[:, :], row_of[:, t:t + 1], None, ALU.is_equal).then_inc(placed[0], 1)
            link(dve.memset(expert_f[:, :], 0.0))
            for e in range(NX):
                link(dve.scalar_tensor_tensor(expert_f[:, :], c.count[0:1, 0:FT], cum[0:1, e:e + 1], expert_f[:, :],
                                              ALU.is_ge, ALU.add))
            link(dve.tensor_scalar(expert_f[:, :], expert_f[:, :], float(NX - 1), None, ALU.min))
            link(dve.tensor_copy(c.expert[:, :], expert_f[:, :]))
            dve.wait_ge(listed, NT)
            link(dve.tensor_copy(listed_f[:, 2], ps_list[:, 0]))
            link(dve.tensor_tensor(listed_f[:, 2], listed_f[:, 2], ps_list[:, 1], ALU.add))
            link(dve.tensor_scalar(listed_f[:, 0], listed_f[:, 2], 0.0, float(NT * P), ALU.is_equal, ALU.mult))
            link(dve.scalar_tensor_tensor(listed_f[:, 1], listed_f[:, 2], -1.0, listed_f[:, 0], ALU.add, ALU.add))
            link(dve.tensor_copy(c.nodes[:, :], listed_f[:, 1]))

        @block.tensor
        def _(pe):
            pe.wait_ge(chosen_ready, 1)
            flat = chosen[:, :, :].rearrange("p t e -> p (t e)")
            pe.matmul(ps_in[:, :], c.upper16[:, :], flat, start=True, stop=True)
            pe.matmul(ps_tot[:, :], c.ones16[:, :], flat, start=True, stop=True).then_inc(counted, 1)
            for t in range(NT):
                pe.wait_ge(placed[t % 2], t // 2 + 1)
                pe.wait_ge(valued, t + 1)
                pe.matmul(ps_list[:, :, :].rearrange("p a n -> p (a n)"), place[:, t % R],
                          value[:, t % R].rearrange("p a n -> p (a n)"), start=t == 0, stop=t == NT - 1).then_inc(listed, 1)


def ffn_phase(nc, c, f, x1_rows, y):
    R = 8
    HC = HID // P
    with ExitStack() as ctx:
        sb, ps, sem = tensors(nc, ctx, "ffn")
        rows = sb("rows", [P, R, XROW])
        xn = sb("xn", [P, 2, D])
        xT = sb("xT", [P, 2, D])
        h = sb("h", [P, 2, HID])
        hT = sb("hT", [P, 2, HID])
        yo = sb("yo", [P, 2, D])
        ps_x = [ps(f"x{i}", [P, D]) for i in range(2)]
        ps_h = ps("h", [P, 2, HID])
        ps_t = ps("t", [P, 2, HID])
        ps_y = [ps(f"y{i}", [P, D]) for i in range(2)]
        gathered = [sem(f"gathered{i}") for i in range(R)]
        y_out = [sem(f"y_out{i}") for i in range(2)]
        xn_ready, x_turned, xT_ready, h_done, h_ready = sem("xn_ready"), sem("x_turned"), sem("xT_ready"), sem("h_done"), sem("h_ready")
        h_turned, hT_ready, y_done, y_ready, ordered = sem("h_turned"), sem("hT_ready"), sem("y_done"), sem("y_ready"), sem("ordered")
        block = ctx.enter_context(nc.Block())

        exists = below(FT)

        @block.gpsimd
        def _(pool):
            def gather(t):
                if t >= R:
                    pool.wait_ge(y_ready, t - R + 1)
                pool.indirect_dma_start(out=rows[:, t % R], out_offset=None, in_=x1_rows,
                                        in_offset=bass.IndirectOffsetOnAxis(ap=c.nodes[:, t:t + 1], axis=0)).then_inc(gathered[t % R], 16)

            for t in range(R):
                gather(t)
            for t in range(FT):
                pool.wait_ge(y_ready, t + 1)
                pool.indirect_dma_start(out=y, out_offset=bass.IndirectOffsetOnAxis(ap=c.nodes[:, t:t + 1], axis=0),
                                        in_=yo[:, t % 2], in_offset=None, bounds_check=N - 1,
                                        oob_is_err=False).then_inc(y_out[t % 2], 16)
                if t + R < FT:
                    gather(t + R)
            pool.wait_ge(y_out[0], 16 * (FT // 2))
            pool.wait_ge(y_out[1], 16 * (FT // 2))

        @block.vector
        def _(dve):
            link = Chain(dve, ordered)

            def normalise(t, r, turn):
                dve.wait_ge(gathered[r], 16 * (turn + 1))
                wait(dve, x_turned, t - 1)
                dve.tensor_scalar(xn[:, r % 2], rows[:, r, 0:D], rows[:, r, D:D + 1], rows[:, r, D + 1:XROW],
                                  ALU.subtract, ALU.mult).then_inc(xn_ready, 1)

            def hidden(t, s, e):
                dve.wait_ge(h_done, t + 1)
                wait(dve, h_turned, t - 1)
                dve.tensor_tensor(h[:, s], ps_h[:, s], f.b1b[:, bass.ds(e * HID, HID)], ALU.add).then_inc(h_ready, 1)

            def result(t, r, e, turn):
                s = r % 2
                dve.wait_ge(y_done, t + 1)
                wait(dve, y_out[s], 16 * turn)
                link(dve.tensor_tensor(yo[:, s], ps_y[s][:, :], f.b2b[:, bass.ds(e * D, D)], ALU.add))
                dve.tensor_tensor(yo[:, s], yo[:, s], rows[:, r, 0:D], ALU.add).then_inc(y_ready, 1)

            def expert(t):
                return dve.value_load(c.expert[0:1, bass.ds(t, 1)], min_val=0, max_val=NX - 1)

            dve.wait_ge(f.loaded, 16 * (2 + 2 * NX))
            for t in range(3):
                normalise(t, t, 0)
            hidden(0, 0, expert(0))

            ahead = {}

            def step(t, r, k):
                if exists(t + 3):
                    normalise(t + 3, (r + 3) % R, k + (r + 3) // R)
                e = ahead.pop(r, None)
                if e is None:
                    e = expert(t)
                if exists(t + 1):
                    following = expert(t + 1)
                    hidden(t + 1, (r + 1) % 2, following)
                    if r < R - 1:
                        ahead[r + 1] = following
                result(t, r, e, R // 2 * k + r // 2)

            tiles(dve, link, FT, R, step)

        @block.scalar
        def _(act):
            def copy(t, s):
                act.wait_ge(x_turned, t + 1)
                wait(act, h_done, t - 1)
                act.copy(xT[:, s], ps_x[s][:, :]).then_inc(xT_ready, 1)

            def relu(t, s):
                act.wait_ge(h_turned, t + 1)
                wait(act, y_done, t - 1)
                act.activation(hT[:, s], ps_t[:, s], ACT.Relu).then_inc(hT_ready, 1)

            copy(0, 0)
            copy(1, 1)

            def step(t, r, k):
                relu(t, r % 2)
                if exists(t + 2):
                    copy(t + 2, r % 2)

            tiles(act, None, FT, R, step)

        @block.tensor
        def _(pe):
            def turn_x(t, s):
                pe.wait_ge(xn_ready, t + 1)
                wait(pe, xT_ready, t - 1)
                for k in range(KC):
                    ins = pe.transpose(ps_x[s][:, k * P:(k + 1) * P], xn[:, s, k * P:(k + 1) * P], c.ident[:, :])
                ins.then_inc(x_turned, 1)

            def first(t, s, e):
                pe.wait_ge(xT_ready, t + 1)
                wait(pe, h_ready, t - 1)
                for k in range(KC):
                    ins = pe.matmul(ps_h[:, s], xT[:, s, k * P:(k + 1) * P], f.w1[:, k, bass.ds(e * HID, HID)],
                                    start=k == 0, stop=k == KC - 1)
                ins.then_inc(h_done, 1)

            def turn_h(t, s):
                pe.wait_ge(h_ready, t + 1)
                wait(pe, hT_ready, t - 1)
                for k in range(HC):
                    ins = pe.transpose(ps_t[:, s, k * P:(k + 1) * P], h[:, s, k * P:(k + 1) * P], c.ident[:, :])
                ins.then_inc(h_turned, 1)

            def second(t, s, e):
                pe.wait_ge(hT_ready, t + 1)
                wait(pe, y_ready, t - 1)
                for k in range(HC):
                    ins = pe.matmul(ps_y[s][:, :], hT[:, s, k * P:(k + 1) * P], f.w2[:, k, bass.ds(e * D, D)],
                                    start=k == 0, stop=k == HC - 1)
                ins.then_inc(y_done, 1)

            def expert(t):
                return pe.value_load(c.expert[0:1, bass.ds(t, 1)], min_val=0, max_val=NX - 1)

            pe.wait_ge(f.loaded, 16 * (2 + 2 * NX))
            turn_x(0, 0)
            turn_x(1, 1)
            first(0, 0, expert(0))

            ahead = {}

            def step(t, r, k):
                turn_h(t, r % 2)
                if exists(t + 2):
                    turn_x(t + 2, r % 2)
                e = ahead.pop(r, None)
                if e is None:
                    e = expert(t)
                if exists(t + 1):
                    following = expert(t + 1)
                    first(t + 1, (r + 1) % 2, following)
                    if r < R - 1:
                        ahead[r + 1] = following
                second(t, r % 2, e)

            tiles(pe, None, FT, R, step)


class Shared:

    def __init__(self, nc, ctx):
        sb = lambda name, shape, dt=F32: ctx.enter_context(nc.sbuf_tensor(name, shape, dt))
        self.lane_i = sb("lane_i", [P, P], I32)
        self.part_i = sb("part_i", [P, 1], I32)
        self.step_i = sb("step_i", [P, SCH], I32)
        self.count_i = sb("count_i", [P, STEPS + 1], I32)
        self.lane = sb("lane", [P, P])
        self.part = sb("part", [P, 1])
        self.step = sb("step", [P, SCH])
        self.count = sb("count", [P, STEPS + 1])
        self.ones = sb("ones", [P, P])
        self.zeros_bf = sb("zeros_bf", [P, D], BF16)
        self.junk = sb("junk", [1, 2])
        self.eps = sb("eps", [P, 1])
        self.ident = sb("ident", [P, P])
        self.upper16 = sb("upper16", [P, P], BF16)
        self.ones16 = sb("ones16", [P, P], BF16)
        self.logit = sb("logit", [P, NT * 2 * H])
        self.logit3 = sb("logit3", [P, (NT + 1) * 3 * 2 * H], BF16)
        self.step_src = sb("step_src", [P, SCH * P], I32)
        self.step_dst = sb("step_dst", [P, SCH * P])
        self.control = sb("control", [1, NWORD + 2], I32)
        self.block_of_step = sb("block_of_step", [1, STEPS], I32)
        self.route = sb("route", [P, NT * NX])
        self.nodes = sb("nodes", [P, FT], I32)
        self.expert = sb("expert", [1, FT], I32)


class ProjectionWeights:

    def __init__(self, nc, ctx):
        sb = lambda name, shape: ctx.enter_context(nc.sbuf_tensor(name, shape, F32))
        self.proj = sb("proj", [P, KC, PROJ])
        self.bias = sb("bias", [P, PROJ])
        self.wlog = sb("wlog", [P, 2, KC, D])
        self.blog = sb("blog", [P, 2, D])
        self.attn = sb("attn", [P, 2, D])


class StepRows:

    def __init__(self, nc, ctx):
        self.rows = ctx.enter_context(nc.sbuf_tensor("step_rows", [P, 2, SCH, P], I32))
        self.block_start = ctx.enter_context(nc.sbuf_tensor("block_start", [P, SCH], F32))
        self.rows_in = ctx.enter_context(nc.semaphore("step_rows_in"))


class FfnWeights:

    def __init__(self, nc, ctx):
        sb = lambda name, shape: ctx.enter_context(nc.sbuf_tensor(name, shape, F32))
        self.w1 = sb("w1", [P, KC, NX * HID])
        self.w2 = sb("w2", [P, HID // P, NX * D])
        self.b1b = sb("b1b", [P, NX * HID])
        self.b2b = sb("b2b", [P, NX * D])
        self.loaded = ctx.enter_context(nc.semaphore("ffn_weights_loaded"))


def gnn_ffn(nc, x, src, dst, W_src, b_src, W_dst, b_dst, W_val, b_val, attn_l, attn_r, Wr, br, W1, b1, W2, b2, y):
    table = nc.dram_tensor("node_table", (NT * P, ROW), F32).ap()
    src_pad = nc.dram_tensor("src_pad", (EPAD,), I32).ap()
    dst_pad = nc.dram_tensor("dst_pad", (EPAD,), I32).ap()
    sums = nc.dram_tensor("sums", (NT * P, SUM), F32).ap()
    x1_rows = nc.dram_tensor("x1_rows", (NT * P, XROW), F32).ap()
    with ExitStack() as ctx:
        c = Shared(nc, ctx)
        constants(nc, c)
        with ExitStack() as preparation:
            w, t = ProjectionWeights(nc, preparation), StepRows(nc, preparation)
            edge_phase(nc, c, w, t, src, dst, W_src, b_src, W_dst, b_dst, W_val, b_val, attn_l, attn_r, src_pad, dst_pad)
            node_phase(nc, c, w, x, table)
            shift_phase(nc, c, t, table)
        message_phase(nc, c, table, sums)
        node_update_phase(nc, c, x, sums, x1_rows, Wr, br)
        f = FfnWeights(nc, ctx)
        route_phase(nc, c, f, W1, b1, W2, b2)
        ffn_phase(nc, c, f, x1_rows, y)


_INS = ["x", "src", "dst"] + ["L0_gnn_" + n for n in ("W_src", "b_src", "W_dst", "b_dst", "W_val", "b_val", "attn_l", "attn_r")] \
    + ["L0_ffn_" + n for n in ("Wr", "br", "W1", "b1", "W2", "b2")]


def kernel(**inputs):
    import numpy as np
    import concourse.bacc as bacc
    from concourse.bass_utils import run_bass_kernel_spmd

    nc = bacc.Bacc("TRN2", target_bir_lowering=False, num_devices=1)
    arrays, args = {}, []
    for name in _INS:
        a = np.ascontiguousarray(inputs[name])
        arrays[f"in_{name}"] = a
        args.append(nc.dram_tensor(f"in_{name}", a.shape, mybir.dt.from_np(a.dtype), kind="ExternalInput").ap())
    out = nc.dram_tensor("out_0", (N, D), F32, kind="ExternalOutput").ap()
    gnn_ffn(nc, *args, out)
    return run_bass_kernel_spmd(nc, [arrays], core_ids=[0]).results[0]["out_0"]
```
